# Optimizing a Trainium2 kernel written in Bass

```python
import numpy as np
import jax
import jax.numpy as jnp

def _softmax(x, axis=-1):
    return jax.nn.softmax(x, axis=axis)

def _gelu(x):
    return jax.nn.gelu(x, approximate=True)

def _silu(x):
    return jax.nn.silu(x)

def _sigmoid(x):
    return jax.nn.sigmoid(x)

def _layernorm(x, axis=-1, eps=1e-05):
    m = jnp.mean(x, axis=axis, keepdims=True)
    v = jnp.var(x, axis=axis, keepdims=True)
    return (x - m) / jnp.sqrt(v + eps)

def _scatter_add(tgt, idx, src, axis=0):
    return tgt.at[idx].add(src)

def _segment_sum(src, seg, n):
    return jax.ops.segment_sum(src, seg, n)
kernel_name = 'mk_xattn_ffn_d1_seqx_r4_1a9166'

def setup_inputs(seed: int=0):
    np.random.seed(seed)
    _w = jnp.asarray

    def _rec_inputs():
        import jax
        import jax.numpy as jnp
        _rk = jax.random.key(seed)
        x = -0.0002928 + 1 * jax.random.normal(jax.random.fold_in(_rk, 1), (16, 100, 256), jnp.float32)
        _lenS = 100 - jax.random.randint(jax.random.fold_in(_rk, 7), (16,), 0, max(1, 100 // 4) + 1, jnp.int32)
        _lenS2 = 361 - jax.random.randint(jax.random.fold_in(_rk, 8), (16,), 0, max(1, 361 // 4) + 1, jnp.int32)
        _ctx_768P = jax.random.normal(jax.random.fold_in(_rk, 11), (16, 16, 192), jnp.float32)
        _ctx_768c = jax.random.dirichlet(jax.random.fold_in(_rk, 511), 0.3 * jnp.ones((16,), jnp.float32), (16, 361))
        _ctx_768t = jnp.einsum('bsk,bkd->bsd', _ctx_768c, _ctx_768P)
        _ctx_768t = _ctx_768t * jax.lax.rsqrt(jnp.mean(jnp.square(_ctx_768t)) + 1e-12) * 0.953939
        ctx_768 = 2.09791e-05 + 1.00001 * (_ctx_768t + 0.3 * jax.random.normal(jax.random.fold_in(_rk, 611), (16, 361, 192), jnp.float32))
        return (x, ctx_768)
    x, ctx_768 = _rec_inputs()

    def _L0_xattn_setup():
        import jax, jax.numpy as jnp
        import numpy as np
        B, LQ, LKV = (2, 512, 512)
        C, CTX, H, DK = (256, 192, 16, 64)
        SCALE = DK ** (-0.5)
        key = jax.random.key(seed)
        kx, ky, kq, kkv, kp, kb = jax.random.split(key, 6)
        return {'x': jax.random.normal(kx, (B, LQ, C), dtype=jnp.float32), 'y': jax.random.normal(ky, (B, LKV, CTX), dtype=jnp.float32), 'Wq': jax.random.normal(kq, (C, H * DK), dtype=jnp.float32) * C ** (-0.5), 'Wkv': jax.random.normal(kkv, (CTX, 2 * H * DK), dtype=jnp.float32) * CTX ** (-0.5), 'Wproj': jax.random.normal(kp, (H * DK, C), dtype=jnp.float32) * (H * DK) ** (-0.5), 'bproj': jax.random.normal(kb, (C,), dtype=jnp.float32) * 0.01}
    _L0_xattn_all = _L0_xattn_setup()
    _L0_xattn_in = {k: v for k, v in _L0_xattn_all.items() if k in ('Wq', 'Wkv', 'Wproj', 'bproj')}
    del _L0_xattn_all

    def _L0_ffn_setup():
        import jax, jax.numpy as jnp
        import numpy as np
        B, T, C, I, E = (4, 512, 256, 704, 7)

        def _swiglu(h, w1, w2, w3):
            return jax.nn.silu(h @ w1.T) * (h @ w3.T) @ w2.T
        key = jax.random.key(seed)
        ks = jax.random.split(key, 9)
        sc_c = 1.0 / np.sqrt(C)
        sc_i = 1.0 / np.sqrt(I)
        return {'x': jax.random.normal(ks[0], (B, T, C), jnp.float32), 'router_w': jax.random.normal(ks[1], (E, C), jnp.float32) * sc_c, 'routing_bias': jnp.zeros((E,), jnp.float32), 'sw1': jax.random.normal(ks[2], (I, C), jnp.float32) * sc_c, 'sw2': jax.random.normal(ks[3], (C, I), jnp.float32) * sc_i, 'sw3': jax.random.normal(ks[4], (I, C), jnp.float32) * sc_c, 'ew1': jax.random.normal(ks[5], (E, I, C), jnp.float32) * sc_c, 'ew2': jax.random.normal(ks[6], (E, C, I), jnp.float32) * sc_i, 'ew3': jax.random.normal(ks[7], (E, I, C), jnp.float32) * sc_c}
    _L0_ffn_all = _L0_ffn_setup()
    _L0_ffn_in = {k: v for k, v in _L0_ffn_all.items() if k in ('router_w', 'routing_bias', 'sw1', 'sw2', 'sw3', 'ew1', 'ew2', 'ew3')}
    del _L0_ffn_all
    return {'x': x, 'ctx_768': ctx_768, 'L0_xattn_Wq': _L0_xattn_in['Wq'], 'L0_xattn_Wkv': _L0_xattn_in['Wkv'], 'L0_xattn_Wproj': _L0_xattn_in['Wproj'], 'L0_xattn_bproj': _L0_xattn_in['bproj'], 'L0_ffn_router_w': _L0_ffn_in['router_w'], 'L0_ffn_routing_bias': _L0_ffn_in['routing_bias'], 'L0_ffn_sw1': _L0_ffn_in['sw1'], 'L0_ffn_sw2': _L0_ffn_in['sw2'], 'L0_ffn_sw3': _L0_ffn_in['sw3'], 'L0_ffn_ew1': _L0_ffn_in['ew1'], 'L0_ffn_ew2': _L0_ffn_in['ew2'], 'L0_ffn_ew3': _L0_ffn_in['ew3']}

def reference(x, ctx_768, L0_xattn_Wq, L0_xattn_Wkv, L0_xattn_Wproj, L0_xattn_bproj, L0_ffn_router_w, L0_ffn_routing_bias, L0_ffn_sw1, L0_ffn_sw2, L0_ffn_sw3, L0_ffn_ew1, L0_ffn_ew2, L0_ffn_ew3):
    import jax
    import jax.numpy as jnp

    def _L0_xattn_ref(x, y, Wq, Wkv, Wproj, bproj):
        import jax, jax.numpy as jnp
        import numpy as np
        B, LQ, LKV = (2, 512, 512)
        C, CTX, H, DK = (256, 192, 16, 64)
        SCALE = DK ** (-0.5)
        b, lq, _ = x.shape
        lkv = y.shape[1]
        q = (x @ Wq).reshape(b, lq, H, DK).transpose(0, 2, 1, 3)
        kv = (y @ Wkv).reshape(b, lkv, 2, H, DK).transpose(2, 0, 3, 1, 4)
        k, v = (kv[0], kv[1])
        atten = jax.nn.softmax(jnp.einsum('bhid,bhjd->bhij', q, k) * SCALE, axis=-1)
        res = jnp.einsum('bhij,bhjd->bhid', atten, v)
        res = res.transpose(0, 2, 1, 3).reshape(b, lq, H * DK)
        out = res @ Wproj + bproj
        return out

    def _L0_ffn_ref(x, router_w, routing_bias, sw1, sw2, sw3, ew1, ew2, ew3):
        import jax, jax.numpy as jnp
        import numpy as np
        B, T, C, I, E = (4, 512, 256, 704, 7)

        def _swiglu(h, w1, w2, w3):
            return jax.nn.silu(h @ w1.T) * (h @ w3.T) @ w2.T
        b, t, c = x.shape
        shared_out = _swiglu(x, sw1, sw2, sw3)
        logits = jnp.clip(x @ router_w.T + routing_bias, -50.0, 50.0)
        probs = jax.nn.sigmoid(logits)
        num_switched = 1
        topk_probs, topk_idx = jax.lax.top_k(probs, num_switched)
        topk_probs = jnp.clip(topk_probs, 1e-08, 1.0 - 1e-08)
        xf = x.reshape(-1, c)
        sel = topk_idx.reshape(-1)
        p = topk_probs.reshape(-1)
        switched = jnp.zeros_like(xf)
        n_experts = ew1.shape[0]
        for e in range(n_experts):
            y = _swiglu(xf, ew1[e], ew2[e], ew3[e])
            w = jnp.where(sel == e, p, 0.0)
            switched = switched + w[:, None] * y
        switched = switched.reshape(b, t, c)
        total_weight = 0.5 + topk_probs.sum(axis=-1)
        total_weight = jnp.clip(total_weight[..., None] + 1e-08, 0.5, 2.0)
        return 0.5 / total_weight * shared_out + switched / total_weight
    x = x + _L0_xattn_ref(_layernorm(x, axis=-1), ctx_768, L0_xattn_Wq, L0_xattn_Wkv, L0_xattn_Wproj, L0_xattn_bproj)
    x = x + _L0_ffn_ref(_layernorm(x, axis=-1), L0_ffn_router_w, L0_ffn_routing_bias, L0_ffn_sw1, L0_ffn_sw2, L0_ffn_sw3, L0_ffn_ew1, L0_ffn_ew2, L0_ffn_ew3)
    return x

_drawn_inputs = setup_inputs


def setup_inputs(seed=0):
    import zlib

    import numpy as np

    out = dict(_drawn_inputs(seed))
    spreads = {'L0_ffn_routing_bias': (0.0, 0.1)}
    factors = {}
    for name, (base, spread) in spreads.items():
        noise = np.random.default_rng([zlib.crc32(name.encode()), seed]).standard_normal(out[name].shape)
        drawn = base * np.exp(spread * noise) if base else spread * noise
        out[name] = jnp.asarray(drawn.astype(out[name].dtype))
    for name, factor in factors.items():
        out[name] = (out[name] * factor).astype(out[name].dtype)
    return out
```

```python
from contextlib import ExitStack

import numpy as np
import concourse.bass as bass
from concourse import mybir

F32 = mybir.dt.float32
F32R = mybir.dt.float32r
U32 = mybir.dt.uint32
I32 = mybir.dt.int32
ACT = mybir.ActivationFunctionType
ALU = mybir.AluOpType
AX = mybir.AxisListType

B, LQ, C = 16, 100, 256
LKV, CTX = 361, 192
H, DK = 16, 64
HD = H * DK
PAIRS = H // 2
STEPS = B * PAIRS
PER = 2 * PAIRS
CC = C // 128
LKE = LKV + 1
KT = 121
NKT = 3
LKP = KT * NKT
LKA = LKP + 1
SCALE = float(DK) ** -0.5
EPS = 1e-5
VU = 2 * NKT

E, I = 7, 704
IC = 6
IM = 640
IR = I - IM
T = 128
NT = (B * LQ + E * (T - 1)) // T
W13 = 2 * I
WROW = CC * W13 + IC * C
XW = C + 2
CHB = 4
CHN = CHB * LQ
CHUNKS = B // CHB
NC_ = (B * LQ + T - 1) // T
SATURATED = 16.64
SKIP = 8192.0
PARTS = dict(tri=LQ, ones=LQ, desc=E, jt=NC_, before=E * E, upto=E * E, tidx=NT, ids=B)
CN = sum(PARTS.values())


def const_slice(cst, name):
    at = 0
    for k, n in PARTS.items():
        if k == name:
            return cst[:, at:at + n]
        at += n


def constants():
    q = np.arange(LQ)
    e = np.arange(E)
    row = dict(desc=E - e, jt=T * np.arange(NC_), before=T * (e[None, :] < e[:, None]).reshape(-1),
               upto=(e[None, :] <= e[:, None]).reshape(-1), tidx=np.arange(NT))
    full = {k: np.broadcast_to(v, (LQ, v.size)) for k, v in row.items()}
    full |= dict(tri=q[:, None] < q[None, :], ones=np.ones((LQ, LQ)), ids=q[:, None] + LQ * np.arange(B)[None, :] + 1)
    return np.concatenate([full[k].astype(np.float32) for k in PARTS], axis=1)


def build(nc, x, ylay, wq, wkv, wproj, bproj, eye, router, rbias, experts, consts, out):
    xs_dram = nc.dram_tensor("xs_dram", (NT * T, XW), F32, kind="Internal").ap()
    with ExitStack() as ctx:
        def sb(name, shape, dt=F32):
            return ctx.enter_context(nc.sbuf_tensor(name, shape, dt))

        def sem(name):
            return ctx.enter_context(nc.semaphore(name))

        ident = sb("ident", [128, 128])
        x_sb = sb("x_sb", [LQ, B, C])
        bp_sb = sb("bp_sb", [LQ, C])
        xnT = sb("xnT", [128, CC, B * LQ])
        w_sh = sb("w_sh", [128, WROW])
        expo = sb("expo", [LQ, B])
        stats = sb("stats", [LQ, B, 6])
        mv = sb("mv", [LQ, B, 2])
        rstd = sb("rstd", [LQ, B])
        router_sb = sb("router_sb", [128, CC, E])
        rb_sb = sb("rb_sb", [LQ, E])
        cst = sb("cst", [LQ, CN])
        attention = ctx.enter_context(ExitStack())

        def sb(name, shape, dt=F32):
            return attention.enter_context(nc.sbuf_tensor(name, shape, dt))

        wq_sb = sb("wq_sb", [128, CC, HD])
        wp_sb = sb("wp_sb", [128, PAIRS, C])
        w_raw = w_sh[:, 0:4 * HD].rearrange("p (a n) -> p a n", a=2)
        wa_hi = sb("wa_hi", [128, 2 * HD], F32R)
        wa_lo = sb("wa_lo", [128, 2 * HD], F32R)
        wb_hi = sb("wb_hi", [128, 2 * HD], F32R)
        wb_lo = sb("wb_lo", [128, 2 * HD], F32R)
        y_raw = sb("y_raw", [128, 2, 2, LKA])
        ya_hi = sb("ya_hi", [128, 2, LKA], F32R)
        ya_lo = sb("ya_lo", [128, 2, LKA], F32R)
        yb_hl = sb("yb_hl", [128, 2, LKA], F32R)
        kT = sb("kT", [128, H, LKE], F32R)
        q_hi = sb("q_hi", [128, H, LQ], F32R)
        q_lo = sb("q_lo", [128, H, LQ], F32R)
        v_sb = sb("v_sb", [KT, 2, NKT, HD])
        probs = sb("probs", [LQ, 2, 2, LKA])
        nmax = sb("nmax", [LQ, 2, 2])
        rsum = sb("rsum", [LQ, 2, 2])
        rinv = sb("rinv", [LQ, 2, 2])
        pT = sb("pT", [KT, 2, NKT, 2, LQ])
        oT = sb("oT", [128, 2, LQ])

        xn = sb("xn", [LQ, 2, C])
        zeros = sb("zeros", [128, XW])
        one = sb("one", [128, 1])
        attention.close()

        def sb(name, shape, dt=F32):
            return ctx.enter_context(nc.sbuf_tensor(name, shape, dt))

        w_ex = sb("w_ex", [128, E, WROW])
        logit = sb("logit", [LQ, B, E])
        key = sb("key", [LQ, B, E])
        onehot = sb("onehot", [LQ, B, E])
        cum = sb("cum", [LQ, 2, B, E])
        cmp = sb("cmp", [LQ, E, max(NC_, E, NT)])
        tmp = sb("tmp", [LQ, B, E])
        small = sb("small", [LQ, 12, B])
        ntile = sb("ntile", [LQ, 4, E])
        pos = sb("pos", [LQ, B], U32)
        tile_ex = sb("tile_ex", [1, NT], I32)
        tile_exf = sb("tile_exf", [1, NT])
        xr = sb("xr", [LQ, B, XW])
        hT = sb("hT", [128, IC, CHN])
        silu = sb("silu", [128, I])
        xs = sb("xs", [T, 2, XW])
        xsT = sb("xsT", [128, 2, CC, T])
        y_out = sb("y_out", [T, 2, C])
        idx_f = sb("idx_f", [T, 2, 2])
        idx = sb("idx", [T, 2], U32)
        hT_flat = hT[:].rearrange("p m q -> p (m q)")
        h_rt = hT_flat[:, 0:I]
        hT_rt = [hT_flat[:, I + IC * T * i:I + IC * T * (i + 1)].rearrange("p (m q) -> p m q", m=IC) for i in range(2)]

        ps = ctx.enter_context(nc.psum_tensor("ps", [128, 8, 512], F32))
        ps_s, ps_t = ps[:, 0:2, :], ps[:, 2:4, :]
        ps_o, ps_y, ps_kq, ps_v = (ps[:, i, :] for i in range(4, 8))
        QO = 384

        ld_id, ld_x, ld_bp, ld_wq, ld_wkv, ld_wp = (sem(f"ld_{n}") for n in ("id", "x", "bp", "wq", "wkv", "wp"))
        y_loaded = [sem("y_loaded0"), sem("y_loaded1")]
        pads_ready, w_split, y_split = sem("pads_ready"), sem("w_split"), sem("y_split")
        bias_added = sem("bias_added")
        y_step = sem("y_step")
        stat_ready, aggr_ready, rstd_ready, xn_ready = sem("stat_ready"), sem("aggr_ready"), sem("rstd_ready"), sem("xn_ready")
        xt_ready, xnT_ready = sem("xt_ready"), sem("xnT_ready")
        scores_ready, nmax_ready, exp_done, rinv_ready, p_ready = (sem(n) for n in (
            "scores_ready", "nmax_ready", "exp_done", "rinv_ready", "p_ready"))
        pT_in_psum, pT_ready, pv_ready, o_ready, proj_ready, x1_ready = (sem(n) for n in (
            "pT_in_psum", "pT_ready", "pv_ready", "o_ready", "proj_ready", "x1_ready"))
        kq_in_psum, kq_hi_ready, kq_lo_ready, v_in_psum, v_ready = (sem(n) for n in (
            "kq_in_psum", "kq_hi_ready", "kq_lo_ready", "v_in_psum", "v_ready"))
        ld_router, ld_wsh, ld_wex, zero_ready, zero_done = (sem(n) for n in ("ld_router", "ld_wsh", "ld_wex", "zero_ready", "zero_done"))
        stats1, logits_in_psum, lmax_ready, prob_ready, onehot_ready, prefix_ready, tiles_known, pos_ready = (sem(n) for n in (
            "stats1", "logits_in_psum", "lmax_ready", "prob_ready", "onehot_ready", "prefix_ready", "tiles_known", "pos_ready"))
        gu_in_psum, silu_ready, h_ready, down_ready, xacc_ready = (sem(n) for n in (
            "gu_in_psum", "silu_ready", "h_ready", "down_ready", "xacc_ready"))
        base_stored, xs_written, dve_chain = sem("base_stored"), sem("xs_written"), sem("dve_chain")
        xs_loaded, y_added = [sem("xs_loaded0"), sem("xs_loaded1")], [sem("y_added0"), sem("y_added1")]
        xsT_in_psum, xsT_ready, rgu_in_psum, rsilu_ready, rh_ready, rhT_in_psum, rhT_ready, ry_in_psum, ry_ready, idx_ready = (sem(n) for n in (
            "xsT_in_psum", "xsT_ready", "rgu_in_psum", "rsilu_ready", "rh_ready", "rhT_in_psum", "rhT_ready", "ry_in_psum", "ry_ready", "idx_ready"))

        def each_tile(eng, step):
            step(0, 0)
            with eng.Fori(0, (NT - 3) // 2) as i:
                step(i * 2 + 1, 1)
                step(i * 2 + 2, 0)
            step(NT - 2, 1)
            step(NT - 1, 0)
            step(NT, 1)

        def tile_in(t, lag=0):
            return not isinstance(t, int) or 0 <= t - lag < NT

        block = ctx.enter_context(nc.Block())

        def each_step(eng, step, lead_in=None):
            for u in range(PER):
                step(0, u)
            with eng.Fori(1, B // 2 - 1) as it:
                for u in range(PER):
                    step(it, u)
            for u in range(PER + 3):
                step(B // 2 - 1, u)

        def static(it):
            return isinstance(it, int)

        def steps_left(it, u, lag=0):
            return not static(it) or 0 <= it * PER + u - lag < STEPS

        @block.sync
        def _(sp):
            sp.dma_start(x_sb[:], x.rearrange("b q c -> q b c")).then_inc(ld_x, 16)
            sp.dma_start(ident[:], eye).then_inc(ld_id, 16)
            sp.dma_start(w_raw[:], wkv).then_inc(ld_wkv, 16)
            sp.wait_ge(pads_ready, 1)
            sp.dma_start(y_raw[:, 0, :, 0:LKV], ylay[:, 0]).then_inc(y_loaded[0], 16)
            sp.dma_start(wq_sb[:], wq.rearrange("(k p) n -> p k n", p=128)).then_inc(ld_wq, 16)
            sp.dma_start(y_raw[:, 1, :, 0:LKV], ylay[:, 1]).then_inc(y_loaded[1], 16)
            sp.dma_start(bp_sb[:], bproj.partition_broadcast(LQ)).then_inc(ld_bp, 16)
            sp.dma_start(wp_sb[:], wproj.rearrange("(g p) n -> p g n", p=128)).then_inc(ld_wp, 16)

            sp.dma_start(router_sb[:], router.rearrange("(k p) e -> p k e", p=128)).then_inc(ld_router, 16)
            sp.dma_start(rb_sb[:], rbias.partition_broadcast(LQ)).then_inc(ld_router, 16)
            sp.dma_start(cst[:], consts).then_inc(ld_router, 16)
            sp.wait_ge(zero_ready, 1)
            sp.dma_start(xs_dram.rearrange("(t p) c -> p t c", p=T), zeros[:].unsqueeze(1).broadcast_to([T, NT, XW])).then_inc(zero_done, 16)
            sp.wait_ge(w_split, 2)
            sp.dma_start(w_sh[:], experts[0]).then_inc(ld_wsh, 16)

            def load_y(b, par):
                sp.wait_ge(y_split, b - 1)
                sp.dma_start(y_raw[:, par, :, 0:LKV], ylay[:, bass.ds(b, 1)].rearrange("p a k l -> p (a k) l")).then_inc(y_loaded[par], 16)

            with sp.Fori(1, B // 2) as it:
                for par in range(2):
                    load_y(2 * it + par, par)
            sp.wait_ge(x1_ready, B)
            for e in range(E):
                sp.dma_start(w_ex[:, e, :], experts[e + 1]).then_inc(ld_wex, 16)

            def store_base(c):
                sp.wait_ge(xacc_ready, c * CHB + CHB)
                sp.dma_start(out.rearrange("b q c -> q b c")[:, bass.ds(c * CHB, CHB), :], x_sb[:, bass.ds(c * CHB, CHB), :]).then_inc(base_stored, 16)

            with sp.Fori(0, CHUNKS) as c:
                store_base(c)
            sp.wait_ge(xs_written, 16 * B)

            def load_tile(t, par):
                if tile_in(t):
                    if not isinstance(t, int) or t >= 2:
                        sp.wait_ge(ry_ready, t - 1)
                    sp.dma_start(xs[:, par, :], xs_dram[bass.ds(t * T, T), :]).then_inc(xs_loaded[par], 16)

            each_tile(sp, load_tile)

        @block.gpsimd
        def _(pool):
            pool.memset(one[:], 1.0)
            pool.memset(y_raw[:], 0.0)
            pool.memset(probs[:], 0.0).then_inc(pads_ready, 1)
            pool.memset(zeros[:], 0.0).then_inc(zero_ready, 1)

            def split_y(b, par):
                pool.wait_ge(y_loaded[par], 8 * (b - par) + 16)
                pool.tensor_tensor(ya_hi[:, par, :], y_raw[:, par, 0, :], one[:].broadcast_to([128, LKA]), ALU.mult)
                pool.tensor_tensor(yb_hl[:, par, :], y_raw[:, par, 1, :], one[:].broadcast_to([128, LKA]), ALU.mult).then_inc(y_step, 1)
                pool.wait_ge(y_step, 2 * b + 1)
                pool.tensor_tensor(ya_lo[:, par, :], y_raw[:, par, 0, :], ya_hi[:, par, :].bitcast(F32), ALU.subtract).then_inc(y_step, 1)
                pool.wait_ge(y_step, 2 * b + 2)
                pool.tensor_tensor(yb_hl[64:128, par, :], y_raw[64:128, par, 1, :], yb_hl[64:128, par, :].bitcast(F32), ALU.subtract).then_inc(y_split, 1)
                pool.wait_ge(y_split, b + 1)

            pool.wait_ge(ld_wkv, 16)
            pool.tensor_copy(wa_hi[:], w_raw[:, 0, :])
            pool.tensor_copy(wb_hi[:], w_raw[:, 1, :]).then_inc(w_split, 1)
            pool.wait_ge(aggr_ready, 2)
            pool.tensor_tensor(rstd[:], rstd[:], expo[:], ALU.pow).then_inc(rstd_ready, 1)
            pool.wait_ge(w_split, 1)
            pool.tensor_tensor(wa_lo[:], w_raw[:, 0, :], wa_hi[:].bitcast(F32), ALU.subtract)
            pool.tensor_tensor(wb_lo[:], w_raw[:, 1, :], wb_hi[:].bitcast(F32), ALU.subtract).then_inc(w_split, 1)
            split_y(0, 0)
            split_y(1, 1)
            pool.wait_ge(ld_bp, 16)
            pool.wait_ge(xn_ready, B)
            for b in range(B):
                last = pool.tensor_tensor(x_sb[:, b, :], x_sb[:, b, :], bp_sb[:], ALU.add)
            last.then_inc(bias_added, 1)

            def step(it, u):
                n, buf = it * PER + u, u % 2
                if u % PAIRS == 1 and (not static(it) or it * 2 + u // PAIRS + 2 < B):
                    b = it * 2 + u // PAIRS
                    pool.wait_ge(kq_in_psum, PAIRS * b + PAIRS)
                    split_y(b + 2, u // PAIRS)
                if steps_left(it, u):
                    pool.wait_ge(rinv_ready, n + 1)
                    pool.tensor_tensor(probs[:, buf, :, 0:LKV], probs[:, buf, :, 0:LKV], rinv[:, buf, :].unsqueeze(2).broadcast_to([LQ, 2, LKV]), ALU.mult).then_inc(p_ready, 1)

            each_step(pool, step)

            pool.wait_ge(aggr_ready, 4)
            pool.tensor_tensor(rstd[:], rstd[:], expo[:], ALU.pow).then_inc(rstd_ready, 1)
            pool.wait_ge(zero_done, 16)
            pool.wait_ge(pos_ready, 1)
            for b in range(B):
                pool.indirect_dma_start(out=xs_dram, out_offset=bass.IndirectOffsetOnAxis(ap=pos[:, b:b + 1], axis=0),
                                        in_=xr[:, b, :], in_offset=None).then_inc(xs_written, 16)

            def add_tile(t, par):
                if tile_in(t):
                    pool.wait_ge(ry_ready, t + 1)
                    pool.wait_ge(base_stored, 16 * CHUNKS)
                    pool.indirect_dma_start(out=out.rearrange("b q c -> (b q) c"), out_offset=bass.IndirectOffsetOnAxis(ap=idx[:, par:par + 1], axis=0),
                                            in_=y_out[:, par, :], in_offset=None, bounds_check=B * LQ - 1, oob_is_err=False,
                                            compute_op=ALU.add).then_inc(y_added[par], 16)

            for t in range(NT):
                add_tile(t, t % 2)
            pool.wait_ge(y_added[0], 16 * ((NT + 1) // 2))
            pool.wait_ge(y_added[1], 16 * (NT // 2))

        @block.tensor
        def _(pe):
            pe.wait_ge(ld_id, 16)
            for b in range(B):
                pe.wait_ge(xn_ready, b + 1)
                if b >= 2:
                    pe.wait_ge(xnT_ready, b - 1)
                for k in range(CC):
                    last = pe.transpose(ps_t[:, b % 2, k * LQ:(k + 1) * LQ], xn[:, b % 2, k * 128:(k + 1) * 128], ident[:LQ, :LQ])
                last.then_inc(xt_ready, 1)

            def project_kq(b, g, par):
                cols = slice(g * 128, (g + 1) * 128)
                parts = ((wa_lo, ya_hi), (wa_hi, ya_lo), (wb_lo, yb_hl), (wb_hi, yb_hl), (wa_hi, ya_hi))
                for i, (w, y) in enumerate(parts):
                    pe.matmul(ps_kq[:, 0:LKE], w[:, cols], y[:, par, 0:LKE], start=i == 0, stop=i == 4)
                for k in range(CC):
                    last = pe.matmul(ps_kq[:, QO:QO + LQ], wq_sb[:, k, cols], xnT[:, k, bass.ds(b * LQ, LQ)], start=k == 0, stop=k == CC - 1)
                last.then_inc(kq_in_psum, 1)

            def project_v(i, par):
                j, half = i % NKT, i // NKT
                rows, cols = slice(j * KT, (j + 1) * KT), slice(HD + 512 * half, HD + 512 * half + 512)
                parts = ((ya_lo, wa_hi), (ya_hi, wa_lo), (yb_hl, wb_lo), (yb_hl, wb_hi), (ya_hi, wa_hi))
                for m, (y, w) in enumerate(parts):
                    last = pe.matmul(ps_v[:KT, :], y[:, par, rows], w[:, cols], start=m == 0, stop=m == 4)
                last.then_inc(v_in_psum, 1)

            pe.wait_ge(w_split, 2)
            pe.wait_ge(y_split, 1)
            pe.wait_ge(ld_wq, 16)
            pe.wait_ge(xnT_ready, B)
            for g in range(PAIRS):
                if g:
                    pe.wait_ge(kq_lo_ready, g)
                project_kq(0, g, 0)
                if g < VU:
                    if g:
                        pe.wait_ge(v_ready, g)
                    project_v(g, 0)

            def step(it, u):
                n, buf, g = it * PER + u, u % 2, u % PAIRS
                b, par = it * 2 + u // PAIRS, (u // PAIRS) % 2
                more = not static(it) or b + 1 < B
                if steps_left(it, u):
                    if static(it) and n:
                        pe.wait_ge(exp_done, n)
                    elif not static(it):
                        pe.wait_ge(exp_done, n)
                    if not more or (static(it) and it == 0 and u == 0):
                        pe.wait_ge(kq_lo_ready, n + 1)
                    for h in range(2):
                        for m, qq in enumerate((q_lo, q_hi)):
                            last = pe.matmul(ps_s[:LQ, h, 0:LKE], qq[:, 2 * g + h, :], kT[:, 2 * g + h, :], start=m == 0, stop=m == 1)
                    last.then_inc(scores_ready, 1)
                if steps_left(it, u, 2):
                    gv, pv = (u - 2) % PAIRS, ((u - 2) // PAIRS) % 2
                    pe.wait_ge(pT_ready, n - 1)
                    if not (static(it) and n < 3):
                        pe.wait_ge(o_ready, n - 2)
                    if static(it) and n == 2:
                        pe.wait_ge(v_ready, VU)
                    elif gv == 0:
                        pe.wait_ge(v_ready, VU * (it * 2 + u // PAIRS) + VU)
                    for j in range(NKT):
                        last = pe.matmul(ps_o[:, 0:2 * LQ], v_sb[:, pv, j, gv * 128:(gv + 1) * 128], pT[:, buf, j, :, :], start=j == 0, stop=j == NKT - 1)
                    last.then_inc(pv_ready, 1)
                if more and steps_left(it, u):
                    if g == 0:
                        pe.wait_ge(y_split, b + 2)
                    pe.wait_ge(kq_lo_ready, n + PAIRS)
                    project_kq(b + 1, g, 1 - par)
                if steps_left(it, u, 1):
                    pe.wait_ge(p_ready, n)
                    if static(it) and n == 1:
                        pass
                    elif not steps_left(it, u, 2):
                        pe.wait_ge(pT_ready, n - 1)
                    for h in range(2):
                        for j in range(NKT):
                            last = pe.transpose(ps_t[:KT, h, j * LQ:(j + 1) * LQ], probs[:, 1 - buf, h, j * KT:(j + 1) * KT], ident[:LQ, :LQ])
                    last.then_inc(pT_in_psum, 1)
                if more and 1 <= g < 1 + VU:
                    pe.wait_ge(v_ready, VU * (b + 1) + g - 1)
                    project_v(g - 1, 1 - par)
                if steps_left(it, u, 3):
                    go = (u - 3) % PAIRS
                    pe.wait_ge(o_ready, n - 2)
                    if static(it) and n == 3:
                        pe.wait_ge(ld_wp, 16)
                    elif go == 0:
                        pe.wait_ge(x1_ready, it * 2 + (u - 3) // PAIRS)
                    last = pe.matmul(ps_y[:LQ, 0:C], oT[:, 1 - buf, :], wp_sb[:, go, :], start=go == 0, stop=go == PAIRS - 1)
                    if go == PAIRS - 1:
                        last.then_inc(proj_ready, 1)

            each_step(pe, step)

            for b in range(B):
                pe.wait_ge(xn_ready, B + b + 1)
                if b >= 2:
                    pe.wait_ge(xnT_ready, B + b - 1)
                for k in range(CC):
                    last = pe.transpose(ps_t[:, b % 2, k * LQ:(k + 1) * LQ], xr[:, b, k * 128:(k + 1) * 128], ident[:LQ, :LQ])
                last.then_inc(xt_ready, 1)
            pe.wait_ge(ld_router, 48)
            for b in range(B):
                pe.wait_ge(xnT_ready, B + b + 1)
                for k in range(CC):
                    last = pe.matmul(ps[:LQ, 6, b * 8:b * 8 + E], xnT[:, k, b * LQ:(b + 1) * LQ], router_sb[:, k, :], start=k == 0, stop=k == CC - 1)
            last.then_inc(logits_in_psum, 1)
            pe.wait_ge(ld_wsh, 16)

            def shared_up(c, m):
                i = c * IC + m
                if not isinstance(i, int) or i >= 2:
                    pe.wait_ge(h_ready, i - 1)
                bank = 2 * (m % 2)
                for side in range(1 if m == IC - 1 else 2):
                    lo = 2 * IM if m == IC - 1 else side * IM + m * 128
                    for k in range(CC):
                        last = pe.matmul(ps[:, bank + side, 0:CHN], w_sh[:, k * W13 + lo:k * W13 + lo + 128],
                                         xnT[:, k, bass.ds(c * CHN, CHN)], start=k == 0, stop=k == CC - 1)
                last.then_inc(gu_in_psum, 1)

            def shared_down(c, first):
                pe.wait_ge(h_ready, c * IC + IC)
                for j in range(CHB):
                    if not (first and j < 2):
                        pe.wait_ge(xacc_ready, c * CHB + j - 1)
                    for m in range(IC):
                        rows = 128 if m < IC - 1 else IR
                        last = pe.matmul(ps[:LQ, 4 + j % 2, 0:C], hT[:rows, m, j * LQ:(j + 1) * LQ],
                                         w_sh[:rows, CC * W13 + m * C:CC * W13 + (m + 1) * C], start=m == 0, stop=m == IC - 1)
                    last.then_inc(down_ready, 1)

            shared_up(0, 0)
            pe.wait_ge(onehot_ready, 1)
            pe.matmul(ps[:LQ, 7, 0:B * E], const_slice(cst, "tri"), onehot[:].rearrange("p b e -> p (b e)"), start=True, stop=True)
            pe.matmul(ps[:LQ, 7, 128:128 + B * E], const_slice(cst, "ones"), onehot[:].rearrange("p b e -> p (b e)"), start=True, stop=True).then_inc(prefix_ready, 1)
            for m in range(1, IC):
                shared_up(0, m)
            shared_down(0, True)
            with pe.Fori(1, CHUNKS) as c:
                for m in range(IC):
                    shared_up(c, m)
                shared_down(c, False)

            pe.wait_ge(ld_wex, 16 * E)
            pe.wait_ge(xacc_ready, B)

            def transpose_tile(t, par):
                pe.wait_ge(xs_loaded[par], 8 * (t - par) + 16)
                for k in range(CC):
                    last = pe.transpose(ps[:, 6, k * T:(k + 1) * T], xs[:, par, k * 128:(k + 1) * 128], ident[:])
                last.then_inc(xsT_in_psum, 1)

            def expert_of(t):
                return pe.value_load(tile_ex[0:1, bass.ds(t, 1)], min_val=0, max_val=E - 1)

            def routed(t, par):
                if tile_in(t):
                    e = expert_of(t)
                    if not isinstance(t, int) or t > 0:
                        pe.wait_ge(rh_ready, t)
                    pe.wait_ge(xsT_ready, t + 1)
                    for lo, n in ((0, 512), (512, 128), (IM, 384), (IM + 384, 256), (2 * IM, 128)):
                        for k in range(CC):
                            last = pe.matmul(ps[:, lo // 512, lo % 512:lo % 512 + n], xsT[:, par, k, :],
                                             w_ex[:, bass.ds(e, 1), k * W13 + lo:k * W13 + lo + n].rearrange("p o n -> p (o n)"), start=k == 0, stop=k == CC - 1)
                    last.then_inc(rgu_in_psum, 1)
                if tile_in(t, 1):
                    e = expert_of(t - 1)
                    pe.wait_ge(rhT_ready, t)
                    if not isinstance(t, int) or t > 1:
                        pe.wait_ge(ry_ready, t - 1)
                    for m in range(IC):
                        rows = 128 if m < IC - 1 else IR
                        last = pe.matmul(ps[:, 5, 0:C], hT_rt[1 - par][:rows, m, :],
                                         w_ex[:rows, bass.ds(e, 1), CC * W13 + m * C:CC * W13 + (m + 1) * C].rearrange("p o n -> p (o n)"), start=m == 0, stop=m == IC - 1)
                    last.then_inc(ry_in_psum, 1)
                if tile_in(t, -1):
                    transpose_tile(t + 1, 1 - par)
                if tile_in(t):
                    pe.wait_ge(rh_ready, t + 1)
                    for m in range(IC):
                        cols = 128 if m < IC - 1 else IR
                        last = pe.transpose(ps[:cols, 3 + m // 4, (m % 4) * T:(m % 4 + 1) * T], h_rt[:, m * 128:m * 128 + cols], ident[:])
                    last.then_inc(rhT_in_psum, 1)

            transpose_tile(0, 0)
            pe.wait_ge(tiles_known, 1)
            each_tile(pe, routed)

        @block.scalar
        def _(act):
            for b in range(B):
                act.wait_ge(xt_ready, b + 1)
                act.activation(xnT[:, :, b * LQ:(b + 1) * LQ], ps_t[:, b % 2, 0:CC * LQ].rearrange("p (k q) -> p k q", k=CC), ACT.Copy).then_inc(xnT_ready, 1)

            def kq_hi(n1, g):
                act.wait_ge(kq_in_psum, n1)
                for h in range(2):
                    act.activation(kT[0:64, 2 * g + h, :], ps_kq[64 * h:64 * h + 64, 0:LKE], ACT.Copy)
                for h in range(2):
                    for half in range(2):
                        last = act.activation(q_hi[64 * half:64 * half + 64, 2 * g + h, :], ps_kq[64 * h:64 * h + 64, QO:QO + LQ], ACT.Copy, scale=SCALE)
                last.then_inc(kq_hi_ready, 1)

            def v_copy(n1, i, par):
                act.wait_ge(v_in_psum, n1)
                act.activation(v_sb[:, par, i % NKT, 512 * (i // NKT):512 * (i // NKT) + 512], ps_v[:KT, :], ACT.Copy).then_inc(v_ready, 1)

            for g in range(PAIRS):
                kq_hi(g + 1, g)
                if g < VU:
                    v_copy(g + 1, g, 0)

            def step(it, u):
                n, buf, g = it * PER + u, u % 2, u % PAIRS
                b, par = it * 2 + u // PAIRS, (u // PAIRS) % 2
                more = not static(it) or b + 1 < B
                if steps_left(it, u):
                    act.wait_ge(nmax_ready, n + 1)
                    for h in range(2):
                        last = act.activation(probs[:, buf, h, 0:LKV], ps_s[:LQ, h, 0:LKV], ACT.Exp, bias=nmax[:, buf, h:h + 1], scale=1.0, accum_out=rsum[:, buf, h:h + 1])
                    last.then_inc(exp_done, 1)
                if steps_left(it, u, 2):
                    act.wait_ge(pv_ready, n - 1)
                    for h in range(2):
                        last = act.activation(oT[64 * h:64 * h + 64, buf, :], ps_o[64 * h:64 * h + 64, h * LQ:(h + 1) * LQ], ACT.Copy)
                    last.then_inc(o_ready, 1)
                if more and steps_left(it, u):
                    kq_hi(n + PAIRS + 1, g)
                if more and 1 <= g < 1 + VU:
                    v_copy(VU * (b + 1) + g, g - 1, 1 - par)

            each_step(act, step)

            for b in range(B):
                act.wait_ge(xt_ready, B + b + 1)
                act.activation(xnT[:, :, b * LQ:(b + 1) * LQ], ps_t[:, b % 2, 0:CC * LQ].rearrange("p (k q) -> p k q", k=CC), ACT.Copy).then_inc(xnT_ready, 1)
            act.wait_ge(lmax_ready, 1)
            act.activation(small[:, 1, :], small[:, 0, :], ACT.Exp, scale=-1.0).then_inc(prob_ready, 1)

            def shared_silu(c, m):
                i = c * IC + m
                act.wait_ge(gu_in_psum, i + 1)
                if not isinstance(i, int) or i >= 1:
                    act.wait_ge(h_ready, i)
                rows = 128 if m < IC - 1 else IR
                act.activation(silu[:rows, 0:CHN], ps[:rows, 2 * (m % 2), 0:CHN], ACT.Silu).then_inc(silu_ready, 1)

            for m in range(IC):
                shared_silu(0, m)
            with act.Fori(1, CHUNKS) as c:
                for m in range(IC):
                    shared_silu(c, m)
            ps_flat = ps[:].rearrange("p k n -> p (k n)")

            def routed(t, par):
                if tile_in(t, 1):
                    act.wait_ge(rhT_in_psum, t)
                    hT_ps = ps_flat[:, 3 * 512:3 * 512 + IC * T].rearrange("p (m q) -> p m q", m=IC)
                    act.activation(hT_rt[1 - par][:, 0:IC - 1, :], hT_ps[:, 0:IC - 1, :], ACT.Copy)
                    act.activation(hT_rt[1 - par][:IR, IC - 1, :], hT_ps[:IR, IC - 1, :], ACT.Copy).then_inc(rhT_ready, 1)
                if tile_in(t):
                    act.wait_ge(rgu_in_psum, t + 1)
                    if not isinstance(t, int) or t > 0:
                        act.wait_ge(rh_ready, t)
                    act.activation(silu[:, 0:IM], ps_flat[:, 0:IM], ACT.Silu)
                    act.activation(silu[:, IM:I], ps_flat[:, 2 * IM:2 * IM + IR], ACT.Silu).then_inc(rsilu_ready, 1)

            each_tile(act, routed)

        @block.vector
        def _(dve):
            dve.memset(expo[:], -0.5)
            dve.wait_ge(ld_x, 16)
            for b in range(B):
                last = dve.bn_stats(stats[:, b, :], x_sb[:, b, :])
            last.then_inc(stat_ready, 1)
            dve.wait_ge(stat_ready, 1)
            for b in range(B):
                last = dve.bn_aggr(mv[:, b, :], stats[:, b, :])
            last.then_inc(aggr_ready, 1)
            dve.wait_ge(aggr_ready, 1)
            dve.tensor_scalar(rstd[:], mv[:, :, 1], EPS, None, ALU.add).then_inc(aggr_ready, 1)
            dve.wait_ge(rstd_ready, 1)
            for b in range(B):
                if b >= 2:
                    dve.wait_ge(xt_ready, b - 1)
                dve.tensor_scalar(xn[:, b % 2, :], x_sb[:, b, :], mv[:, b, 0:1], rstd[:, b:b + 1], ALU.subtract, ALU.mult).then_inc(xn_ready, 1)

            def kq_lo(n1, g):
                dve.wait_ge(kq_hi_ready, n1)
                for h in range(2):
                    dve.tensor_tensor(kT[64:128, 2 * g + h, :], ps_kq[64 * h:64 * h + 64, 0:LKE], kT[0:64, 2 * g + h, :].bitcast(F32), ALU.subtract)
                for h in range(2):
                    for half in range(2):
                        rows = slice(64 * half, 64 * half + 64)
                        last = dve.scalar_tensor_tensor(q_lo[rows, 2 * g + h, :], ps_kq[64 * h:64 * h + 64, QO:QO + LQ], SCALE, q_hi[rows, 2 * g + h, :].bitcast(F32), ALU.mult, ALU.subtract)
                last.then_inc(kq_lo_ready, 1)

            for g in range(PAIRS):
                kq_lo(g + 1, g)
            dve.wait_ge(pads_ready, 1)

            def step(it, u):
                n, buf, g = it * PER + u, u % 2, u % PAIRS
                b = it * 2 + u // PAIRS
                more = not static(it) or b + 1 < B
                if steps_left(it, u):
                    dve.wait_ge(scores_ready, n + 1)
                    dve.tensor_reduce(nmax[:, buf, :], ps_s[:LQ, :, 0:LKV], AX.X, ALU.max, negate=True).then_inc(nmax_ready, 1)
                    dve.wait_ge(exp_done, n + 1)
                    dve.reciprocal(rinv[:, buf, :], rsum[:, buf, :]).then_inc(rinv_ready, 1)
                if steps_left(it, u, 1):
                    dve.wait_ge(pT_in_psum, n)
                    dve.tensor_copy(pT[:, 1 - buf, :, :, :].rearrange("p j h q -> p h j q"), ps_t[:KT, :, 0:NKT * LQ].rearrange("p h (j q) -> p h j q", j=NKT)).then_inc(pT_ready, 1)
                if more and steps_left(it, u):
                    kq_lo(n + PAIRS + 1, g)
                if steps_left(it, u, 3) and (u - 3) % PAIRS == PAIRS - 1:
                    bo = it * 2 + (u - 3) // PAIRS
                    dve.wait_ge(proj_ready, bo + 1)
                    if static(it) and it == 0 and u == PAIRS + 2:
                        dve.wait_ge(bias_added, 1)
                    dve.tensor_tensor(x_sb[:, bass.ds(bo, 1), :].rearrange("p o c -> p (o c)"), x_sb[:, bass.ds(bo, 1), :].rearrange("p o c -> p (o c)"), ps_y[:LQ, 0:C], ALU.add).then_inc(x1_ready, 1)
                    dve.wait_ge(x1_ready, bo + 1)
                    dve.bn_stats(stats[:, bass.ds(bo, 1), :].rearrange("p o s -> p (o s)"), x_sb[:, bass.ds(bo, 1), :].rearrange("p o c -> p (o c)")).then_inc(stats1, 1)

            each_step(dve, step)

            def link(ins):
                chain[0] += 1
                ins.then_inc(dve_chain, 1)
                dve.wait_ge(dve_chain, chain[0])

            chain = [0]
            dve.wait_ge(stats1, B)
            for b in range(B):
                last = dve.bn_aggr(mv[:, b, :], stats[:, b, :])
            last.then_inc(aggr_ready, 1)
            dve.wait_ge(aggr_ready, 3)
            dve.tensor_scalar(rstd[:], mv[:, :, 1], EPS, None, ALU.add).then_inc(aggr_ready, 1)
            dve.wait_ge(rstd_ready, 2)
            for b in range(B):
                dve.tensor_scalar(xr[:, b, 0:C], x_sb[:, b, :], mv[:, b, 0:1], rstd[:, b:b + 1], ALU.subtract, ALU.mult).then_inc(xn_ready, 1)

            def over_e(v):
                return v.unsqueeze(2).broadcast_to([LQ, B, E])

            def over_b(v):
                return v.unsqueeze(1).broadcast_to([LQ, B, E])

            lmax, ex, kmax, dmax, prob, tw, cs, pos_f = (small[:, i, :] for i in range(8))
            desc = const_slice(cst, "desc")
            dve.wait_ge(logits_in_psum, 1)
            link(dve.tensor_tensor(logit[:], ps[:LQ, 6, 0:B * 8].rearrange("p (b e) -> p b e", b=B)[:, :, 0:E], over_b(rb_sb[:]), ALU.add))
            link(dve.tensor_scalar(logit[:], logit[:], 50.0, -50.0, ALU.min, ALU.max))
            dve.tensor_reduce(lmax, logit[:], AX.X, ALU.max).then_inc(lmax_ready, 1)
            dve.wait_ge(lmax_ready, 1)
            dve.tensor_scalar(key[:], logit[:], SATURATED, None, ALU.min)
            link(dve.tensor_scalar(kmax, lmax, SATURATED, None, ALU.min))
            link(dve.tensor_tensor(tmp[:], key[:], over_e(kmax), ALU.is_equal))
            link(dve.tensor_tensor(tmp[:], tmp[:], over_b(desc), ALU.mult))
            link(dve.tensor_reduce(dmax, tmp[:], AX.X, ALU.max))
            dve.tensor_tensor(onehot[:], over_b(desc), over_e(dmax), ALU.is_equal).then_inc(onehot_ready, 1)
            dve.wait_ge(prob_ready, 1)
            link(dve.tensor_scalar(ex, ex, 1.0, None, ALU.add))
            link(dve.reciprocal(prob, ex))
            link(dve.tensor_scalar(prob, prob, 1e-8, 1.0, ALU.max, ALU.min))
            link(dve.tensor_scalar(tw, prob, 0.5, 1e-8, ALU.add, ALU.add))
            link(dve.tensor_scalar(tw, tw, 0.5, 2.0, ALU.max, ALU.min))
            link(dve.reciprocal(tw, tw))
            link(dve.tensor_scalar(cs, tw, 0.5, None, ALU.mult))
            link(dve.tensor_tensor(xr[:, :, C], prob, tw, ALU.mult))
            link(dve.tensor_copy(xr[:, :, C + 1], const_slice(cst, "ids")))
            dve.wait_ge(prefix_ready, 1)
            before = ps[:LQ, 7, 0:B * E].rearrange("p (b e) -> p b e", b=B)
            count = ps[:LQ, 7, 128:128 + B * E].rearrange("p (b e) -> p b e", b=B)
            link(dve.tensor_copy(cum[:, 0], count))
            side, s = 0, 1
            while s < B:
                dve.tensor_copy(cum[:, 1 - side, 0:s, :], cum[:, side, 0:s, :])
                link(dve.tensor_tensor(cum[:, 1 - side, s:B, :], cum[:, side, s:B, :], cum[:, side, 0:B - s, :], ALU.add))
                side, s = 1 - side, 2 * s
            upto, ranks = cum[:, side], cum[:, 1 - side]
            tiles, start_row, end_tile = (ntile[:, i, :] for i in range(3))
            link(dve.tensor_tensor(cmp[:, :, 0:NC_], upto[:, B - 1, :].unsqueeze(2).broadcast_to([LQ, E, NC_]),
                                   const_slice(cst, "jt").unsqueeze(1).broadcast_to([LQ, E, NC_]), ALU.is_gt))
            link(dve.tensor_reduce(tiles, cmp[:, :, 0:NC_], AX.X, ALU.add))
            for name, to in (("before", start_row), ("upto", end_tile)):
                link(dve.tensor_tensor(cmp[:, :, 0:E], const_slice(cst, name).rearrange("p (a b) -> p a b", a=E),
                                       tiles.unsqueeze(1).broadcast_to([LQ, E, E]), ALU.mult))
                link(dve.tensor_reduce(to, cmp[:, :, 0:E], AX.X, ALU.add))
            over = cmp[:].rearrange("p a b -> p (a b)")[0:1, 0:NT * E].rearrange("p (t e) -> p t e", t=NT)
            link(dve.tensor_tensor(over, end_tile[0:1].unsqueeze(1).broadcast_to([1, NT, E]),
                                   const_slice(cst, "tidx")[0:1].unsqueeze(2).broadcast_to([1, NT, E]), ALU.is_le))
            link(dve.tensor_reduce(tile_exf[:], over, AX.X, ALU.add))
            dve.tensor_scalar(tile_ex[:], tile_exf[:], float(E - 1), None, ALU.min).then_inc(tiles_known, 1)
            link(dve.tensor_tensor(ranks, upto, before, ALU.add))
            link(dve.tensor_tensor(ranks, ranks, count, ALU.subtract))
            link(dve.tensor_tensor(ranks, ranks, over_b(start_row), ALU.add))
            link(dve.tensor_tensor(ranks, ranks, onehot[:], ALU.mult))
            link(dve.tensor_reduce(pos_f, ranks, AX.X, ALU.add))
            dve.tensor_copy(pos[:], pos_f).then_inc(pos_ready, 1)

            def shared_h(c, m):
                dve.wait_ge(silu_ready, c * IC + m + 1)
                if m < IC - 1:
                    dve.tensor_tensor(hT[:, m, :], silu[:, 0:CHN], ps[:, 2 * (m % 2) + 1, 0:CHN], ALU.mult).then_inc(h_ready, 1)
                else:
                    dve.tensor_tensor(hT[:IR, m, :], silu[:IR, 0:CHN], ps[IR:128, 2 * (m % 2), 0:CHN], ALU.mult).then_inc(h_ready, 1)

            def shared_acc(c):
                for j in range(CHB):
                    b = c * CHB + j
                    dve.wait_ge(down_ready, b + 1)
                    x_b = x_sb[:, bass.ds(b, 1), :].rearrange("p o c -> p (o c)")
                    dve.scalar_tensor_tensor(x_b, ps[:LQ, 4 + j % 2, 0:C], cs[:, bass.ds(b, 1)], x_b, ALU.mult, ALU.add).then_inc(xacc_ready, 1)

            with dve.Fori(0, CHUNKS) as c:
                for m in range(IC):
                    shared_h(c, m)
                shared_acc(c)
            ps_flat = ps[:].rearrange("p k n -> p (k n)")

            def tile_in_T(t, par):
                dve.wait_ge(xsT_in_psum, t + 1)
                dve.tensor_copy(xsT[:, par, :, :], ps[:, 6, 0:CC * T].rearrange("p (k q) -> p k q", k=CC)).then_inc(xsT_ready, 1)

            def routed(t, par):
                if tile_in(t, 1):
                    o = 1 - par
                    dve.wait_ge(ry_in_psum, t)
                    if not isinstance(t, int) or t > 2:
                        dve.wait_ge(y_added[o], 8 * (t - 1 - o))
                    dve.tensor_scalar(idx_f[:, o, 0:1], xs[:, o, C + 1:C + 2], 0.0, SKIP, ALU.is_equal, ALU.mult)
                    dve.tensor_scalar(y_out[:, o, :], ps[:, 5, 0:C], xs[:, o, C:C + 1], None, ALU.mult).then_inc(idx_ready, 1)
                    dve.wait_ge(idx_ready, t)
                    dve.scalar_tensor_tensor(idx[:, o:o + 1], xs[:, o, C + 1:C + 2], -1.0, idx_f[:, o, 0:1], ALU.add, ALU.add).then_inc(ry_ready, 1)
                if tile_in(t, -1):
                    tile_in_T(t + 1, 1 - par)
                if tile_in(t):
                    dve.wait_ge(rsilu_ready, t + 1)
                    dve.tensor_tensor(h_rt[:, 0:IM], silu[:, 0:IM], ps_flat[:, IM:2 * IM], ALU.mult)
                    dve.tensor_tensor(h_rt[:, IM:I], silu[:, IM:I], ps_flat[:, 2 * IM + IR:W13], ALU.mult).then_inc(rh_ready, 1)

            tile_in_T(0, 0)
            each_tile(dve, routed)


def lay_expert(w1, w2, w3):
    up = np.concatenate([w1[:IM], w3[:IM], w1[IM:], w3[IM:]]).T
    down = np.zeros((IC * 128, C), w2.dtype)
    down[:I] = w2.T
    return np.concatenate([up.reshape(CC, 128, W13).transpose(1, 0, 2).reshape(128, -1),
                           down.reshape(IC, 128, C).transpose(1, 0, 2).reshape(128, -1)], axis=1)


def kernel(**inputs):
    import numpy as _np
    import concourse.bacc as _bacc
    from concourse import mybir as _mybir
    from concourse.bass_utils import run_bass_kernel_spmd as _run
    nc = _bacc.Bacc("TRN2", target_bir_lowering=False, num_devices=1)
    a = {k: _np.asarray(v) for k, v in inputs.items()}
    yT = a["ctx_768"].transpose(2, 0, 1)
    wkv = a["L0_xattn_Wkv"]
    arrays = {
        "x": a["x"],
        "ylay": _np.stack([yT[:128], _np.concatenate([yT[128:], yT[128:]])], axis=2),
        "wq": a["L0_xattn_Wq"],
        "wkv": _np.stack([wkv[:128], _np.concatenate([wkv[128:], wkv[128:]])], axis=1),
        "wproj": a["L0_xattn_Wproj"], "bproj": a["L0_xattn_bproj"],
        "eye": _np.eye(128, dtype=_np.float32),
        "router": a["L0_ffn_router_w"].T, "rbias": a["L0_ffn_routing_bias"],
        "experts": _np.stack([lay_expert(*(a[f"L0_ffn_sw{i}"] for i in (1, 2, 3)))]
                             + [lay_expert(*(a[f"L0_ffn_ew{i}"][e] for i in (1, 2, 3))) for e in range(E)]),
        "consts": constants(),
    }
    arrays = {k: _np.ascontiguousarray(v) for k, v in arrays.items()}
    args = [nc.dram_tensor(k, v.shape, _mybir.dt.from_np(v.dtype), kind="ExternalInput").ap() for k, v in arrays.items()]
    out = nc.dram_tensor("out", (B, LQ, C), F32, kind="ExternalOutput").ap()
    build(nc, *args, out)
    r = _run(nc, [arrays], core_ids=[0])
    return r.results[0]["out"]
```

```python
from contextlib import ExitStack

import numpy as np
import concourse.bass as bass
from concourse import mybir

F32 = mybir.dt.float32
F32R = mybir.dt.float32r
U32 = mybir.dt.uint32
I32 = mybir.dt.int32
ACT = mybir.ActivationFunctionType
ALU = mybir.AluOpType
AX = mybir.AxisListType

B, LQ, C = 16, 100, 256
LKV, CTX = 361, 192
H, DK = 16, 64
HD = H * DK
PAIRS = H // 2
STEPS = B * PAIRS
PER = 2 * PAIRS
CC = C // 128
LKE = LKV + 1
KT = 121
NKT = 3
LKP = KT * NKT
LKA = LKP + 1
SCALE = float(DK) ** -0.5
EPS = 1e-5
VU = 2 * NKT
GROUPS = ((0, 4), (4, B))
LATE = {0: [1], 1: [2], 2: [3], 4: [4, 5, 6], 5: [7, 8, 9], 6: [10, 11, 12], 7: [13, 14, 15]}

E, I = 7, 704
IC = 6
IM = 640
IR = I - IM
T = 128
NT = (B * LQ + E * (T - 1)) // T
W13 = 2 * I
WROW = CC * W13 + IC * C
XW = C + 2
CHB = 4
CHN = CHB * LQ
CHUNKS = B // CHB
NC_ = (B * LQ + T - 1) // T
SATURATED = 16.64
SKIP = 8192.0
PARTS = dict(tri=LQ, ones=LQ, desc=E, jt=NC_, before=E * E, upto=E * E, tidx=NT, ids=B)
CN = sum(PARTS.values())


def const_slice(cst, name):
    at = 0
    for k, n in PARTS.items():
        if k == name:
            return cst[:, at:at + n]
        at += n


def constants():
    q = np.arange(LQ)
    e = np.arange(E)
    row = dict(desc=E - e, jt=T * np.arange(NC_), before=T * (e[None, :] < e[:, None]).reshape(-1),
               upto=(e[None, :] <= e[:, None]).reshape(-1), tidx=np.arange(NT))
    full = {k: np.broadcast_to(v, (LQ, v.size)) for k, v in row.items()}
    full |= dict(tri=q[:, None] < q[None, :], ones=np.ones((LQ, LQ)), ids=q[:, None] + LQ * np.arange(B)[None, :] + 1)
    return np.concatenate([full[k].astype(np.float32) for k in PARTS], axis=1)


def build(nc, x, ylay, wq, wkv, wproj, bproj, eye, router, rbias, experts, consts, out):
    xs_dram = nc.dram_tensor("xs_dram", (NT * T, XW), F32, kind="Internal").ap()
    with ExitStack() as ctx:
        def sb(name, shape, dt=F32):
            return ctx.enter_context(nc.sbuf_tensor(name, shape, dt))

        def sem(name):
            return ctx.enter_context(nc.semaphore(name))

        ident = sb("ident", [128, 128])
        x_sb = sb("x_sb", [LQ, B, C])
        bp_sb = sb("bp_sb", [LQ, C])
        xnT = sb("xnT", [128, CC, B * LQ])
        w_sh = sb("w_sh", [128, WROW])
        expo = sb("expo", [LQ, B])
        stats = sb("stats", [LQ, B, 6])
        mv = sb("mv", [LQ, B, 2])
        rstd = sb("rstd", [LQ, B])
        router_sb = sb("router_sb", [128, CC, E])
        rb_sb = sb("rb_sb", [LQ, E])
        cst = sb("cst", [LQ, CN])
        attention = ctx.enter_context(ExitStack())

        def sb(name, shape, dt=F32):
            return attention.enter_context(nc.sbuf_tensor(name, shape, dt))

        wq_sb = sb("wq_sb", [128, CC, HD])
        wp_sb = sb("wp_sb", [128, PAIRS, C])
        w_raw = w_sh[:, 0:4 * HD].rearrange("p (v a n) -> p v a n", v=2, a=2)
        w_hi = sb("w_hi", [128, 2, 2, HD], F32R)
        w_lo = sb("w_lo", [128, 2, 2, HD], F32R)
        y_raw = sb("y_raw", [128, 2, 2, LKA])
        ya_hi = sb("ya_hi", [128, 2, LKA], F32R)
        ya_lo = sb("ya_lo", [128, 2, LKA], F32R)
        yb_hl = sb("yb_hl", [128, 2, LKA], F32R)
        kT = sb("kT", [128, H, LKE], F32R)
        q_hi = sb("q_hi", [128, H, LQ], F32R)
        q_lo = sb("q_lo", [128, H, LQ], F32R)
        v_sb = sb("v_sb", [KT, 2, NKT, HD])
        probs = sb("probs", [LQ, 2, 2, LKA])
        nmax = sb("nmax", [LQ, 2, 2])
        rsum = sb("rsum", [LQ, 2, 2])
        rinv = sb("rinv", [LQ, 2, 2])
        pT = sb("pT", [KT, 2, NKT, 2, LQ])
        oT = sb("oT", [128, 2, LQ])

        xn = sb("xn", [LQ, 2, C])
        zeros = sb("zeros", [128, XW])
        one = sb("one", [128, 1])
        attention.close()

        def sb(name, shape, dt=F32):
            return ctx.enter_context(nc.sbuf_tensor(name, shape, dt))

        w_ex = sb("w_ex", [128, E, WROW])
        logit = sb("logit", [LQ, B, E])
        key = sb("key", [LQ, B, E])
        onehot = sb("onehot", [LQ, B, E])
        cum = sb("cum", [LQ, 2, B, E])
        cmp = sb("cmp", [LQ, E, max(NC_, E, NT)])
        tmp = sb("tmp", [LQ, B, E])
        small = sb("small", [LQ, 12, B])
        ntile = sb("ntile", [LQ, 4, E])
        pos = sb("pos", [LQ, B], U32)
        tile_ex = sb("tile_ex", [1, NT], I32)
        tile_exf = sb("tile_exf", [1, NT])
        xr = sb("xr", [LQ, B, XW])
        hT = sb("hT", [128, IC, CHN])
        silu = sb("silu", [128, I])
        xs = sb("xs", [T, 2, XW])
        xsT = sb("xsT", [128, 2, CC, T])
        y_out = sb("y_out", [T, 2, C])
        idx_f = sb("idx_f", [T, 2, 2])
        meta_in = sb("meta_in", [T, 2, 2])
        meta = sb("meta", [T, 2, 2])
        idx = sb("idx", [T, 2], U32)
        hT_flat = hT[:].rearrange("p m q -> p (m q)")
        h_rt = hT_flat[:, 0:I]
        hT_rt = [hT_flat[:, I + IC * T * i:I + IC * T * (i + 1)].rearrange("p (m q) -> p m q", m=IC) for i in range(2)]

        ps = ctx.enter_context(nc.psum_tensor("ps", [128, 8, 512], F32))
        ps_s, ps_t = ps[:, 0:2, :], ps[:, 2:4, :]
        ps_o, ps_y, ps_kq, ps_v = (ps[:, i, :] for i in range(4, 8))
        QO = 384

        ld_id, ld_bp, ld_wq, ld_wp = (sem(f"ld_{n}") for n in ("id", "bp", "wq", "wp"))
        ld_x = [sem(f"ld_x{i}") for i in range(4)]
        ld_wkv = [sem("ld_wk"), sem("ld_wv")]
        w_rounded = sem("w_rounded")
        y_loaded = [sem("y_loaded0"), sem("y_loaded1")]
        pads_ready, w_split, y_split = sem("pads_ready"), sem("w_split"), sem("y_split")
        bias_added = sem("bias_added")
        y_step = sem("y_step")
        stat_ready, aggr_ready, rstd_ready, xn_ready = sem("stat_ready"), sem("aggr_ready"), sem("rstd_ready"), sem("xn_ready")
        xt_ready, xnT_ready = sem("xt_ready"), sem("xnT_ready")
        scores_ready, nmax_ready, exp_done, rinv_ready, p_ready = (sem(n) for n in (
            "scores_ready", "nmax_ready", "exp_done", "rinv_ready", "p_ready"))
        pT_in_psum, pT_ready, pv_ready, o_ready, proj_ready, x1_ready = (sem(n) for n in (
            "pT_in_psum", "pT_ready", "pv_ready", "o_ready", "proj_ready", "x1_ready"))
        kq_in_psum, kq_hi_ready, kq_lo_ready, v_in_psum, v_ready = (sem(n) for n in (
            "kq_in_psum", "kq_hi_ready", "kq_lo_ready", "v_in_psum", "v_ready"))
        ld_router, ld_wsh, ld_wex, zero_ready, zero_done = (sem(n) for n in ("ld_router", "ld_wsh", "ld_wex", "zero_ready", "zero_done"))
        stats1, logits_in_psum, lmax_ready, prob_ready, onehot_ready, prefix_ready, tiles_known, pos_ready = (sem(n) for n in (
            "stats1", "logits_in_psum", "lmax_ready", "prob_ready", "onehot_ready", "prefix_ready", "tiles_known", "pos_ready"))
        gu_in_psum, silu_ready, h_ready, down_ready, xacc_ready = (sem(n) for n in (
            "gu_in_psum", "silu_ready", "h_ready", "down_ready", "xacc_ready"))
        base_stored, xs_written, dve_chain = sem("base_stored"), sem("xs_written"), sem("dve_chain")
        xs_loaded, y_added = [sem("xs_loaded0"), sem("xs_loaded1")], [sem("y_added0"), sem("y_added1")]
        xsT_in_psum, xsT_ready, rgu_in_psum, rsilu_ready, rh_ready, rhT_in_psum, rhT_ready, ry_in_psum, ry_ready, idx_ready = (sem(n) for n in (
            "xsT_in_psum", "xsT_ready", "rgu_in_psum", "rsilu_ready", "rh_ready", "rhT_in_psum", "rhT_ready", "ry_in_psum", "ry_ready", "idx_ready"))

        def each_tile(eng, step):
            step(0, 0)
            with eng.Fori(0, (NT - 3) // 2) as i:
                step(i * 2 + 1, 1)
                step(i * 2 + 2, 0)
            step(NT - 2, 1)
            step(NT - 1, 0)
            step(NT, 1)

        def tile_in(t, lag=0):
            return not isinstance(t, int) or 0 <= t - lag < NT

        block = ctx.enter_context(nc.Block())

        def each_step(eng, step, lead_in=None):
            for u in range(PER):
                step(0, u)
            with eng.Fori(1, B // 2 - 1) as it:
                for u in range(PER):
                    step(it, u)
            for u in range(PER + 3):
                step(B // 2 - 1, u)

        def static(it):
            return isinstance(it, int)

        def steps_left(it, u, lag=0):
            return not static(it) or 0 <= it * PER + u - lag < STEPS

        @block.sync
        def _(sp):
            sp.dma_start(w_raw[:, 1], wkv[:, 1]).then_inc(ld_wkv[1], 16)
            sp.dma_start(w_raw[:, 0], wkv[:, 0]).then_inc(ld_wkv[0], 16)
            sp.dma_start(ident[:], eye).then_inc(ld_id, 16)
            sp.dma_start(wq_sb[:], wq.rearrange("(k p) n -> p k n", p=128)).then_inc(ld_wq, 16)
            for i in range(1, 4):
                sp.dma_start(x_sb[:, 4 * i:4 * i + 4, :], x.rearrange("b q c -> q b c")[:, 4 * i:4 * i + 4, :]).then_inc(ld_x[i], 16)
            sp.dma_start(y_raw[:, 1], ylay[:, 1]).then_inc(y_loaded[1], 16)
            sp.dma_start(bp_sb[:], bproj.partition_broadcast(LQ)).then_inc(ld_bp, 16)
            sp.dma_start(wp_sb[:], wproj.rearrange("(g p) n -> p g n", p=128)).then_inc(ld_wp, 16)
            sp.dma_start(router_sb[:], router.rearrange("(k p) e -> p k e", p=128)).then_inc(ld_router, 16)
            sp.dma_start(rb_sb[:], rbias.partition_broadcast(LQ)).then_inc(ld_router, 16)
            sp.dma_start(cst[:], consts).then_inc(ld_router, 16)
            sp.wait_ge(w_split, 2)
            sp.dma_start(w_sh[:], experts[0]).then_inc(ld_wsh, 16)
            sp.wait_ge(zero_ready, 1)
            sp.dma_start(xs_dram.rearrange("(t p) c -> p t c", p=T), zeros[:].unsqueeze(1).broadcast_to([T, NT, XW])).then_inc(zero_done, 16)

            def load_y(b, par):
                sp.wait_ge(y_split, b - 1)
                sp.dma_start(y_raw[:, par], ylay[:, bass.ds(b, 1)].rearrange("p a k l -> p (a k) l")).then_inc(y_loaded[par], 16)

            with sp.Fori(1, B // 2) as it:
                for par in range(2):
                    load_y(2 * it + par, par)
            sp.wait_ge(x1_ready, B)
            for e in range(E):
                sp.dma_start(w_ex[:, e, :], experts[e + 1]).then_inc(ld_wex, 16)

            def store_base(c):
                sp.wait_ge(xacc_ready, c * CHB + CHB)
                sp.dma_start(out.rearrange("b q c -> q b c")[:, bass.ds(c * CHB, CHB), :], x_sb[:, bass.ds(c * CHB, CHB), :]).then_inc(base_stored, 16)

            with sp.Fori(0, CHUNKS) as c:
                store_base(c)
            sp.wait_ge(xs_written, 16 * B)

            def load_tile(t, par):
                if tile_in(t):
                    if not isinstance(t, int) or t >= 2:
                        sp.wait_ge(xsT_ready, t - 1)
                    sp.dma_start(xs[:, par, :], xs_dram[bass.ds(t * T, T), :]).then_inc(xs_loaded[par], 16)

            each_tile(sp, load_tile)

        @block.gpsimd
        def _(pool):
            pool.memset(one[:], 1.0)
            pool.memset(probs[:, :, :, LKV:LKA], 0.0).then_inc(pads_ready, 1)
            pool.memset(zeros[:], 0.0).then_inc(zero_ready, 1)
            pool.wait_ge(zero_ready, 1)

            def split_y(b, par):
                pool.wait_ge(y_loaded[par], 8 * (b - par) + 16)
                pool.tensor_tensor(ya_hi[:, par, :], y_raw[:, par, 0, :], one[:].broadcast_to([128, LKA]), ALU.mult)
                pool.tensor_tensor(yb_hl[:, par, :], y_raw[:, par, 1, :], one[:].broadcast_to([128, LKA]), ALU.mult).then_inc(y_step, 1)
                pool.wait_ge(y_step, 2 * b + 1)
                pool.tensor_tensor(ya_lo[:, par, :], y_raw[:, par, 0, :], ya_hi[:, par, :].bitcast(F32), ALU.subtract).then_inc(y_step, 1)
                pool.wait_ge(y_step, 2 * b + 2)
                pool.tensor_tensor(yb_hl[64:128, par, :], y_raw[64:128, par, 1, :], yb_hl[64:128, par, :].bitcast(F32), ALU.subtract).then_inc(y_split, 1)
                pool.wait_ge(y_split, b + 1)

            split_y(0, 0)
            for i, (lo, hi) in enumerate(GROUPS):
                pool.wait_ge(aggr_ready, 2 * i + 2)
                pool.tensor_tensor(rstd[:, lo:hi], rstd[:, lo:hi], expo[:, lo:hi], ALU.pow).then_inc(rstd_ready, 1)
            split_y(1, 1)
            pool.wait_ge(ld_bp, 16)
            pool.wait_ge(xn_ready, B)
            for b in range(B):
                last = pool.tensor_tensor(x_sb[:, b, :], x_sb[:, b, :], bp_sb[:], ALU.add)
            last.then_inc(bias_added, 1)

            def step(it, u):
                n, buf = it * PER + u, u % 2
                if u % PAIRS == 1 and (not static(it) or it * 2 + u // PAIRS + 2 < B):
                    b = it * 2 + u // PAIRS
                    pool.wait_ge(kq_in_psum, PAIRS * b + PAIRS)
                    split_y(b + 2, u // PAIRS)
                if steps_left(it, u):
                    pool.wait_ge(rinv_ready, n + 1)
                    pool.tensor_tensor(probs[:, buf, :, 0:LKV], probs[:, buf, :, 0:LKV], rinv[:, buf, :].unsqueeze(2).broadcast_to([LQ, 2, LKV]), ALU.mult).then_inc(p_ready, 1)

            each_step(pool, step)

            pool.wait_ge(aggr_ready, 6)
            pool.tensor_tensor(rstd[:], rstd[:], expo[:], ALU.pow).then_inc(rstd_ready, 1)
            pool.wait_ge(zero_done, 16)
            pool.wait_ge(pos_ready, 1)
            for b in range(B):
                pool.indirect_dma_start(out=xs_dram, out_offset=bass.IndirectOffsetOnAxis(ap=pos[:, b:b + 1], axis=0),
                                        in_=xr[:, b, :], in_offset=None).then_inc(xs_written, 16)

            def add_tile(t, par):
                if tile_in(t):
                    pool.wait_ge(ry_ready, t + 1)
                    pool.wait_ge(base_stored, 16 * CHUNKS)
                    pool.indirect_dma_start(out=out.rearrange("b q c -> (b q) c"), out_offset=bass.IndirectOffsetOnAxis(ap=idx[:, par:par + 1], axis=0),
                                            in_=y_out[:, par, :], in_offset=None, bounds_check=B * LQ - 1, oob_is_err=False,
                                            compute_op=ALU.add).then_inc(y_added[par], 16)

            for t in range(NT):
                add_tile(t, t % 2)
            pool.wait_ge(y_added[0], 16 * ((NT + 1) // 2))
            pool.wait_ge(y_added[1], 16 * (NT // 2))

        @block.tensor
        def _(pe):
            pe.wait_ge(ld_id, 16)

            def transpose_x(b):
                pe.wait_ge(xn_ready, b + 1)
                if b >= 2:
                    pe.wait_ge(xnT_ready, b - 1)
                for k in range(CC):
                    last = pe.transpose(ps_t[:, b % 2, k * LQ:(k + 1) * LQ], xn[:, b % 2, k * 128:(k + 1) * 128], ident[:LQ, :LQ])
                last.then_inc(xt_ready, 1)

            def project_kq(b, g, par, acc=ps_kq):
                cols = slice(g * 128, (g + 1) * 128)
                parts = ((w_lo, 0, ya_hi), (w_hi, 0, ya_lo), (w_lo, 1, yb_hl), (w_hi, 1, yb_hl), (w_hi, 0, ya_hi))
                for i, (w, a, y) in enumerate(parts):
                    pe.matmul(acc[:, 0:LKE], w[:, 0, a, cols], y[:, par, 0:LKE], start=i == 0, stop=i == 4)
                for k in range(CC):
                    last = pe.matmul(acc[:, QO:QO + LQ], wq_sb[:, k, cols], xnT[:, k, bass.ds(b * LQ, LQ)], start=k == 0, stop=k == CC - 1)
                last.then_inc(kq_in_psum, 1)

            def project_v(i, par):
                j, half = i % NKT, i // NKT
                rows, cols = slice(j * KT, (j + 1) * KT), slice(512 * half, 512 * half + 512)
                parts = ((ya_lo, w_hi, 0), (ya_hi, w_lo, 0), (yb_hl, w_lo, 1), (yb_hl, w_hi, 1), (ya_hi, w_hi, 0))
                for m, (y, w, a) in enumerate(parts):
                    last = pe.matmul(ps_v[:KT, :], y[:, par, rows], w[:, 1, a, cols], start=m == 0, stop=m == 4)
                last.then_inc(v_in_psum, 1)

            pe.wait_ge(w_split, 1)
            pe.wait_ge(y_split, 1)
            for i in range(VU):
                if i:
                    pe.wait_ge(v_ready, i)
                project_v(i, 0)
            transpose_x(0)
            pe.wait_ge(w_split, 2)
            pe.wait_ge(ld_wq, 16)
            pe.wait_ge(xnT_ready, 1)
            for g in range(PAIRS):
                if g >= 2:
                    pe.wait_ge(kq_lo_ready, g - 1)
                project_kq(0, g, 0, (ps_kq, ps_o)[g % 2])
                for b in LATE.get(g, []):
                    transpose_x(b)

            def step(it, u):
                n, buf, g = it * PER + u, u % 2, u % PAIRS
                b, par = it * 2 + u // PAIRS, (u // PAIRS) % 2
                more = not static(it) or b + 1 < B
                if steps_left(it, u):
                    if static(it) and n:
                        pe.wait_ge(exp_done, n)
                    elif not static(it):
                        pe.wait_ge(exp_done, n)
                    if not more or (static(it) and it == 0 and u == 0):
                        pe.wait_ge(kq_lo_ready, n + 1)
                    for h in range(2):
                        for m, qq in enumerate((q_lo, q_hi)):
                            last = pe.matmul(ps_s[:LQ, h, 0:LKE], qq[:, 2 * g + h, :], kT[:, 2 * g + h, :], start=m == 0, stop=m == 1)
                    last.then_inc(scores_ready, 1)
                if steps_left(it, u, 2):
                    gv, pv = (u - 2) % PAIRS, ((u - 2) // PAIRS) % 2
                    pe.wait_ge(pT_ready, n - 1)
                    if not (static(it) and n < 3):
                        pe.wait_ge(o_ready, n - 2)
                    if static(it) and n == 2:
                        pe.wait_ge(v_ready, VU)
                    elif gv == 0:
                        pe.wait_ge(v_ready, VU * (it * 2 + u // PAIRS) + VU)
                    for j in range(NKT):
                        last = pe.matmul(ps_o[:, 0:2 * LQ], v_sb[:, pv, j, gv * 128:(gv + 1) * 128], pT[:, buf, j, :, :], start=j == 0, stop=j == NKT - 1)
                    last.then_inc(pv_ready, 1)
                if steps_left(it, u, 3):
                    go = (u - 3) % PAIRS
                    pe.wait_ge(o_ready, n - 2)
                    if static(it) and n == 3:
                        pe.wait_ge(ld_wp, 16)
                    elif go == 0:
                        pe.wait_ge(x1_ready, it * 2 + (u - 3) // PAIRS)
                    last = pe.matmul(ps_y[:LQ, 0:C], oT[:, 1 - buf, :], wp_sb[:, go, :], start=go == 0, stop=go == PAIRS - 1)
                    if go == PAIRS - 1:
                        last.then_inc(proj_ready, 1)
                if steps_left(it, u, 1):
                    pe.wait_ge(p_ready, n)
                    if static(it) and n == 1:
                        pass
                    elif not steps_left(it, u, 2):
                        pe.wait_ge(pT_ready, n - 1)
                    for h in range(2):
                        for j in range(NKT):
                            last = pe.transpose(ps_t[:KT, h, j * LQ:(j + 1) * LQ], probs[:, 1 - buf, h, j * KT:(j + 1) * KT], ident[:LQ, :LQ])
                    last.then_inc(pT_in_psum, 1)
                if more and 1 <= g < 1 + VU:
                    pe.wait_ge(v_ready, VU * (b + 1) + g - 1)
                    project_v(g - 1, 1 - par)
                if more and steps_left(it, u):
                    if g == 0:
                        pe.wait_ge(y_split, b + 2)
                    pe.wait_ge(kq_lo_ready, n + PAIRS)
                    project_kq(b + 1, g, 1 - par)

            each_step(pe, step)

            for b in range(B):
                pe.wait_ge(xn_ready, B + b + 1)
                if b >= 2:
                    pe.wait_ge(xnT_ready, B + b - 1)
                for k in range(CC):
                    last = pe.transpose(ps_t[:, b % 2, k * LQ:(k + 1) * LQ], xr[:, b, k * 128:(k + 1) * 128], ident[:LQ, :LQ])
                last.then_inc(xt_ready, 1)
            pe.wait_ge(ld_router, 48)
            for b in range(B):
                pe.wait_ge(xnT_ready, B + b + 1)
                for k in range(CC):
                    last = pe.matmul(ps[:LQ, 6, b * 8:b * 8 + E], xnT[:, k, b * LQ:(b + 1) * LQ], router_sb[:, k, :], start=k == 0, stop=k == CC - 1)
            last.then_inc(logits_in_psum, 1)
            pe.wait_ge(ld_wsh, 16)

            def shared_up(c, m):
                i = c * IC + m
                if not isinstance(i, int) or i >= 2:
                    pe.wait_ge(h_ready, i - 1)
                bank = 2 * (m % 2)
                for side in range(1 if m == IC - 1 else 2):
                    lo = 2 * IM if m == IC - 1 else side * IM + m * 128
                    for k in range(CC):
                        last = pe.matmul(ps[:, bank + side, 0:CHN], w_sh[:, k * W13 + lo:k * W13 + lo + 128],
                                         xnT[:, k, bass.ds(c * CHN, CHN)], start=k == 0, stop=k == CC - 1)
                last.then_inc(gu_in_psum, 1)

            def shared_down(c, first):
                pe.wait_ge(h_ready, c * IC + IC)
                for j in range(CHB):
                    if not (first and j < 2):
                        pe.wait_ge(xacc_ready, c * CHB + j - 1)
                    for m in range(IC):
                        rows = 128 if m < IC - 1 else IR
                        last = pe.matmul(ps[:LQ, 4 + j % 2, 0:C], hT[:rows, m, j * LQ:(j + 1) * LQ],
                                         w_sh[:rows, CC * W13 + m * C:CC * W13 + (m + 1) * C], start=m == 0, stop=m == IC - 1)
                    last.then_inc(down_ready, 1)

            shared_up(0, 0)
            pe.wait_ge(onehot_ready, 1)
            pe.matmul(ps[:LQ, 7, 0:B * E], const_slice(cst, "tri"), onehot[:].rearrange("p b e -> p (b e)"), start=True, stop=True)
            pe.matmul(ps[:LQ, 7, 128:128 + B * E], const_slice(cst, "ones"), onehot[:].rearrange("p b e -> p (b e)"), start=True, stop=True).then_inc(prefix_ready, 1)
            for m in range(1, IC):
                shared_up(0, m)
            shared_down(0, True)
            with pe.Fori(1, CHUNKS) as c:
                for m in range(IC):
                    shared_up(c, m)
                shared_down(c, False)

            pe.wait_ge(ld_wex, 16 * E)
            pe.wait_ge(xacc_ready, B)

            def transpose_tile(t, par):
                pe.wait_ge(xs_loaded[par], 8 * (t - par) + 16)
                for k in range(CC):
                    last = pe.transpose(ps[:, 6, k * T:(k + 1) * T], xs[:, par, k * 128:(k + 1) * 128], ident[:])
                last.then_inc(xsT_in_psum, 1)

            def expert_of(t):
                return pe.value_load(tile_ex[0:1, bass.ds(t, 1)], min_val=0, max_val=E - 1)

            def routed(t, par):
                if tile_in(t):
                    e = expert_of(t)
                    if not isinstance(t, int) or t > 0:
                        pe.wait_ge(rh_ready, t)
                    pe.wait_ge(xsT_ready, t + 1)
                    for lo, n in ((0, 512), (512, 128), (IM, 384), (IM + 384, 256), (2 * IM, 128)):
                        for k in range(CC):
                            last = pe.matmul(ps[:, lo // 512, lo % 512:lo % 512 + n], xsT[:, par, k, :],
                                             w_ex[:, bass.ds(e, 1), k * W13 + lo:k * W13 + lo + n].rearrange("p o n -> p (o n)"), start=k == 0, stop=k == CC - 1)
                    last.then_inc(rgu_in_psum, 1)
                if tile_in(t, -1):
                    transpose_tile(t + 1, 1 - par)
                if tile_in(t, 1):
                    e = expert_of(t - 1)
                    pe.wait_ge(rhT_ready, t)
                    if not isinstance(t, int) or t > 1:
                        pe.wait_ge(ry_ready, t - 1)
                    for m in range(IC):
                        rows = 128 if m < IC - 1 else IR
                        last = pe.matmul(ps[:, 5, 0:C], hT_rt[1 - par][:rows, m, :],
                                         w_ex[:rows, bass.ds(e, 1), CC * W13 + m * C:CC * W13 + (m + 1) * C].rearrange("p o n -> p (o n)"), start=m == 0, stop=m == IC - 1)
                    last.then_inc(ry_in_psum, 1)
                if tile_in(t):
                    pe.wait_ge(rh_ready, t + 1)
                    for m in range(IC):
                        cols = 128 if m < IC - 1 else IR
                        last = pe.transpose(ps[:cols, 3 + m // 4, (m % 4) * T:(m % 4 + 1) * T], h_rt[:, m * 128:m * 128 + cols], ident[:])
                    last.then_inc(rhT_in_psum, 1)

            transpose_tile(0, 0)
            pe.wait_ge(tiles_known, 1)
            each_tile(pe, routed)

        @block.scalar
        def _(act):
            act.dma_start(y_raw[:, 0], ylay[:, 0]).then_inc(y_loaded[0], 16)
            act.dma_start(x_sb[:, 0:4, :], x.rearrange("b q c -> q b c")[:, 0:4, :]).then_inc(ld_x[0], 16)
            for i in (1, 0):
                act.wait_ge(ld_wkv[i], 16)
                act.activation(w_hi[:, i], w_raw[:, i], ACT.Copy).then_inc(w_rounded, 1)

            def copy_xT(b):
                act.wait_ge(xt_ready, b + 1)
                act.activation(xnT[:, :, b * LQ:(b + 1) * LQ], ps_t[:, b % 2, 0:CC * LQ].rearrange("p (k q) -> p k q", k=CC), ACT.Copy).then_inc(xnT_ready, 1)

            def kq_hi(n1, g, acc=ps_kq):
                act.wait_ge(kq_in_psum, n1)
                for h in range(2):
                    act.activation(kT[0:64, 2 * g + h, :], acc[64 * h:64 * h + 64, 0:LKE], ACT.Copy)
                for h in range(2):
                    for half in range(2):
                        last = act.activation(q_hi[64 * half:64 * half + 64, 2 * g + h, :], acc[64 * h:64 * h + 64, QO:QO + LQ], ACT.Copy, scale=SCALE)
                last.then_inc(kq_hi_ready, 1)

            def v_copy(n1, i, par):
                act.wait_ge(v_in_psum, n1)
                act.activation(v_sb[:, par, i % NKT, 512 * (i // NKT):512 * (i // NKT) + 512], ps_v[:KT, :], ACT.Copy).then_inc(v_ready, 1)

            for i in range(VU):
                v_copy(i + 1, i, 0)
            copy_xT(0)
            for g in range(PAIRS):
                kq_hi(g + 1, g, (ps_kq, ps_o)[g % 2])
                for b in LATE.get(g, []):
                    copy_xT(b)

            def step(it, u):
                n, buf, g = it * PER + u, u % 2, u % PAIRS
                b, par = it * 2 + u // PAIRS, (u // PAIRS) % 2
                more = not static(it) or b + 1 < B
                if steps_left(it, u):
                    act.wait_ge(nmax_ready, n + 1)
                    for h in range(2):
                        last = act.activation(probs[:, buf, h, 0:LKV], ps_s[:LQ, h, 0:LKV], ACT.Exp, bias=nmax[:, buf, h:h + 1], scale=1.0, accum_out=rsum[:, buf, h:h + 1])
                    last.then_inc(exp_done, 1)
                if steps_left(it, u, 2):
                    act.wait_ge(pv_ready, n - 1)
                    for h in range(2):
                        last = act.activation(oT[64 * h:64 * h + 64, buf, :], ps_o[64 * h:64 * h + 64, h * LQ:(h + 1) * LQ], ACT.Copy)
                    last.then_inc(o_ready, 1)
                if more and 1 <= g < 1 + VU:
                    v_copy(VU * (b + 1) + g, g - 1, 1 - par)
                if more and steps_left(it, u):
                    kq_hi(n + PAIRS + 1, g)

            each_step(act, step)

            for b in range(B):
                act.wait_ge(xt_ready, B + b + 1)
                act.activation(xnT[:, :, b * LQ:(b + 1) * LQ], ps_t[:, b % 2, 0:CC * LQ].rearrange("p (k q) -> p k q", k=CC), ACT.Copy).then_inc(xnT_ready, 1)
            act.wait_ge(lmax_ready, 1)
            act.activation(small[:, 1, :], small[:, 0, :], ACT.Exp, scale=-1.0).then_inc(prob_ready, 1)

            def shared_silu(c, m):
                i = c * IC + m
                act.wait_ge(gu_in_psum, i + 1)
                if not isinstance(i, int) or i >= 1:
                    act.wait_ge(h_ready, i)
                rows = 128 if m < IC - 1 else IR
                act.activation(silu[:rows, 0:CHN], ps[:rows, 2 * (m % 2), 0:CHN], ACT.Silu).then_inc(silu_ready, 1)

            for m in range(IC):
                shared_silu(0, m)
            with act.Fori(1, CHUNKS) as c:
                for m in range(IC):
                    shared_silu(c, m)
            ps_flat = ps[:].rearrange("p k n -> p (k n)")

            def routed(t, par):
                if tile_in(t, 1):
                    act.wait_ge(rhT_in_psum, t)
                    hT_ps = ps_flat[:, 3 * 512:3 * 512 + IC * T].rearrange("p (m q) -> p m q", m=IC)
                    act.activation(hT_rt[1 - par][:, 0:IC - 1, :], hT_ps[:, 0:IC - 1, :], ACT.Copy)
                    act.activation(hT_rt[1 - par][:IR, IC - 1, :], hT_ps[:IR, IC - 1, :], ACT.Copy).then_inc(rhT_ready, 1)
                if tile_in(t):
                    act.wait_ge(rgu_in_psum, t + 1)
                    if not isinstance(t, int) or t > 0:
                        act.wait_ge(rh_ready, t)
                    act.activation(silu[:, 0:IM], ps_flat[:, 0:IM], ACT.Silu)
                    act.activation(silu[:, IM:I], ps_flat[:, 2 * IM:2 * IM + IR], ACT.Silu).then_inc(rsilu_ready, 1)

            each_tile(act, routed)

        @block.vector
        def _(dve):
            dve.memset(expo[:], -0.5)
            for i in range(2):
                dve.wait_ge(w_rounded, i + 1)
                dve.tensor_tensor(w_lo[:, 1 - i], w_raw[:, 1 - i], w_hi[:, 1 - i].bitcast(F32), ALU.subtract).then_inc(w_split, 1)

            def moments(lo, hi):
                for b in range(lo, hi):
                    last = dve.bn_stats(stats[:, b, :], x_sb[:, b, :])
                last.then_inc(stat_ready, 1)

            def variance(i):
                lo, hi = GROUPS[i]
                for b in range(lo, hi):
                    last = dve.bn_aggr(mv[:, b, :], stats[:, b, :])
                last.then_inc(aggr_ready, 1)
                dve.wait_ge(aggr_ready, 2 * i + 1)
                dve.tensor_scalar(rstd[:, lo:hi], mv[:, lo:hi, 1], EPS, None, ALU.add).then_inc(aggr_ready, 1)

            def normalise(b):
                if b >= 2:
                    dve.wait_ge(xt_ready, b - 1)
                dve.tensor_scalar(xn[:, b % 2, :], x_sb[:, b, :], mv[:, b, 0:1], rstd[:, b:b + 1], ALU.subtract, ALU.mult).then_inc(xn_ready, 1)

            dve.wait_ge(ld_x[0], 16)
            moments(0, 4)
            dve.wait_ge(stat_ready, 1)
            variance(0)
            dve.wait_ge(rstd_ready, 1)
            normalise(0)
            normalise(1)

            def kq_lo(n1, g, acc=ps_kq):
                dve.wait_ge(kq_hi_ready, n1)
                for h in range(2):
                    dve.tensor_tensor(kT[64:128, 2 * g + h, :], acc[64 * h:64 * h + 64, 0:LKE], kT[0:64, 2 * g + h, :].bitcast(F32), ALU.subtract)
                for h in range(2):
                    for half in range(2):
                        rows = slice(64 * half, 64 * half + 64)
                        last = dve.scalar_tensor_tensor(q_lo[rows, 2 * g + h, :], acc[64 * h:64 * h + 64, QO:QO + LQ], SCALE, q_hi[rows, 2 * g + h, :].bitcast(F32), ALU.mult, ALU.subtract)
                last.then_inc(kq_lo_ready, 1)

            for g in range(PAIRS):
                kq_lo(g + 1, g, (ps_kq, ps_o)[g % 2])
                if g < 2:
                    normalise(2 + g)
                if g < 3:
                    dve.wait_ge(ld_x[g + 1], 16)
                    moments(4 * g + 4, 4 * g + 8)
                if g == 2:
                    dve.wait_ge(stat_ready, 4)
                    variance(1)
                    dve.wait_ge(rstd_ready, 2)
                    normalise(4)
                    normalise(5)
                if g >= 4:
                    for b in LATE[g]:
                        if b + 2 < B:
                            normalise(b + 2)
            dve.wait_ge(pads_ready, 1)

            def step(it, u):
                n, buf, g = it * PER + u, u % 2, u % PAIRS
                b = it * 2 + u // PAIRS
                more = not static(it) or b + 1 < B
                if steps_left(it, u):
                    dve.wait_ge(scores_ready, n + 1)
                    dve.tensor_reduce(nmax[:, buf, :], ps_s[:LQ, :, 0:LKV], AX.X, ALU.max, negate=True).then_inc(nmax_ready, 1)
                bp = it * 2 + (u - 1) // PAIRS
                if (not static(it) or bp + 1 < B) and not (static(it) and n == 0):
                    kq_lo(n + PAIRS, (u - 1) % PAIRS)
                if steps_left(it, u):
                    dve.wait_ge(exp_done, n + 1)
                    dve.reciprocal(rinv[:, buf, :], rsum[:, buf, :]).then_inc(rinv_ready, 1)
                if steps_left(it, u, 1):
                    dve.wait_ge(pT_in_psum, n)
                    dve.tensor_copy(pT[:, 1 - buf, :, :, :].rearrange("p j h q -> p h j q"), ps_t[:KT, :, 0:NKT * LQ].rearrange("p h (j q) -> p h j q", j=NKT)).then_inc(pT_ready, 1)
                if steps_left(it, u, 3) and (u - 3) % PAIRS == PAIRS - 1:
                    bo = it * 2 + (u - 3) // PAIRS
                    dve.wait_ge(proj_ready, bo + 1)
                    if static(it) and it == 0 and u == PAIRS + 2:
                        dve.wait_ge(bias_added, 1)
                    dve.tensor_tensor(x_sb[:, bass.ds(bo, 1), :].rearrange("p o c -> p (o c)"), x_sb[:, bass.ds(bo, 1), :].rearrange("p o c -> p (o c)"), ps_y[:LQ, 0:C], ALU.add).then_inc(x1_ready, 1)
                    dve.wait_ge(x1_ready, bo + 1)
                    dve.bn_stats(stats[:, bass.ds(bo, 1), :].rearrange("p o s -> p (o s)"), x_sb[:, bass.ds(bo, 1), :].rearrange("p o c -> p (o c)")).then_inc(stats1, 1)

            each_step(dve, step)

            def link(ins):
                chain[0] += 1
                ins.then_inc(dve_chain, 1)
                dve.wait_ge(dve_chain, chain[0])

            chain = [0]
            dve.wait_ge(stats1, B)
            for b in range(B):
                last = dve.bn_aggr(mv[:, b, :], stats[:, b, :])
            last.then_inc(aggr_ready, 1)
            dve.wait_ge(aggr_ready, 5)
            dve.tensor_scalar(rstd[:], mv[:, :, 1], EPS, None, ALU.add).then_inc(aggr_ready, 1)
            dve.wait_ge(rstd_ready, 3)
            for b in range(B):
                dve.tensor_scalar(xr[:, b, 0:C], x_sb[:, b, :], mv[:, b, 0:1], rstd[:, b:b + 1], ALU.subtract, ALU.mult).then_inc(xn_ready, 1)

            def over_e(v):
                return v.unsqueeze(2).broadcast_to([LQ, B, E])

            def over_b(v):
                return v.unsqueeze(1).broadcast_to([LQ, B, E])

            lmax, ex, kmax, dmax, prob, tw, cs, pos_f = (small[:, i, :] for i in range(8))
            desc = const_slice(cst, "desc")
            dve.wait_ge(logits_in_psum, 1)
            link(dve.tensor_tensor(logit[:], ps[:LQ, 6, 0:B * 8].rearrange("p (b e) -> p b e", b=B)[:, :, 0:E], over_b(rb_sb[:]), ALU.add))
            link(dve.tensor_scalar(logit[:], logit[:], 50.0, -50.0, ALU.min, ALU.max))
            dve.tensor_reduce(lmax, logit[:], AX.X, ALU.max).then_inc(lmax_ready, 1)
            dve.wait_ge(lmax_ready, 1)
            dve.tensor_scalar(key[:], logit[:], SATURATED, None, ALU.min)
            link(dve.tensor_scalar(kmax, lmax, SATURATED, None, ALU.min))
            link(dve.tensor_tensor(tmp[:], key[:], over_e(kmax), ALU.is_equal))
            link(dve.tensor_tensor(tmp[:], tmp[:], over_b(desc), ALU.mult))
            link(dve.tensor_reduce(dmax, tmp[:], AX.X, ALU.max))
            dve.tensor_tensor(onehot[:], over_b(desc), over_e(dmax), ALU.is_equal).then_inc(onehot_ready, 1)
            dve.wait_ge(prob_ready, 1)
            link(dve.tensor_scalar(ex, ex, 1.0, None, ALU.add))
            link(dve.reciprocal(prob, ex))
            link(dve.tensor_scalar(prob, prob, 1e-8, 1.0, ALU.max, ALU.min))
            link(dve.tensor_scalar(tw, prob, 0.5, 1e-8, ALU.add, ALU.add))
            link(dve.tensor_scalar(tw, tw, 0.5, 2.0, ALU.max, ALU.min))
            link(dve.reciprocal(tw, tw))
            link(dve.tensor_scalar(cs, tw, 0.5, None, ALU.mult))
            link(dve.tensor_tensor(xr[:, :, C], prob, tw, ALU.mult))
            link(dve.tensor_copy(xr[:, :, C + 1], const_slice(cst, "ids")))
            dve.wait_ge(prefix_ready, 1)
            before = ps[:LQ, 7, 0:B * E].rearrange("p (b e) -> p b e", b=B)
            count = ps[:LQ, 7, 128:128 + B * E].rearrange("p (b e) -> p b e", b=B)
            link(dve.tensor_copy(cum[:, 0], count))
            side, s = 0, 1
            while s < B:
                dve.tensor_copy(cum[:, 1 - side, 0:s, :], cum[:, side, 0:s, :])
                link(dve.tensor_tensor(cum[:, 1 - side, s:B, :], cum[:, side, s:B, :], cum[:, side, 0:B - s, :], ALU.add))
                side, s = 1 - side, 2 * s
            upto, ranks = cum[:, side], cum[:, 1 - side]
            tiles, start_row, end_tile = (ntile[:, i, :] for i in range(3))
            link(dve.tensor_tensor(cmp[:, :, 0:NC_], upto[:, B - 1, :].unsqueeze(2).broadcast_to([LQ, E, NC_]),
                                   const_slice(cst, "jt").unsqueeze(1).broadcast_to([LQ, E, NC_]), ALU.is_gt))
            link(dve.tensor_reduce(tiles, cmp[:, :, 0:NC_], AX.X, ALU.add))
            for name, to in (("before", start_row), ("upto", end_tile)):
                link(dve.tensor_tensor(cmp[:, :, 0:E], const_slice(cst, name).rearrange("p (a b) -> p a b", a=E),
                                       tiles.unsqueeze(1).broadcast_to([LQ, E, E]), ALU.mult))
                link(dve.tensor_reduce(to, cmp[:, :, 0:E], AX.X, ALU.add))
            over = cmp[:].rearrange("p a b -> p (a b)")[0:1, 0:NT * E].rearrange("p (t e) -> p t e", t=NT)
            link(dve.tensor_tensor(over, end_tile[0:1].unsqueeze(1).broadcast_to([1, NT, E]),
                                   const_slice(cst, "tidx")[0:1].unsqueeze(2).broadcast_to([1, NT, E]), ALU.is_le))
            link(dve.tensor_reduce(tile_exf[:], over, AX.X, ALU.add))
            dve.tensor_scalar(tile_ex[:], tile_exf[:], float(E - 1), None, ALU.min).then_inc(tiles_known, 1)
            link(dve.tensor_tensor(ranks, upto, before, ALU.add))
            link(dve.tensor_tensor(ranks, ranks, count, ALU.subtract))
            link(dve.tensor_tensor(ranks, ranks, over_b(start_row), ALU.add))
            link(dve.tensor_tensor(ranks, ranks, onehot[:], ALU.mult))
            link(dve.tensor_reduce(pos_f, ranks, AX.X, ALU.add))
            dve.tensor_copy(pos[:], pos_f).then_inc(pos_ready, 1)

            def shared_h(c, m):
                dve.wait_ge(silu_ready, c * IC + m + 1)
                if m < IC - 1:
                    dve.tensor_tensor(hT[:, m, :], silu[:, 0:CHN], ps[:, 2 * (m % 2) + 1, 0:CHN], ALU.mult).then_inc(h_ready, 1)
                else:
                    dve.tensor_tensor(hT[:IR, m, :], silu[:IR, 0:CHN], ps[IR:128, 2 * (m % 2), 0:CHN], ALU.mult).then_inc(h_ready, 1)

            def shared_acc(c):
                for j in range(CHB):
                    b = c * CHB + j
                    dve.wait_ge(down_ready, b + 1)
                    x_b = x_sb[:, bass.ds(b, 1), :].rearrange("p o c -> p (o c)")
                    dve.scalar_tensor_tensor(x_b, ps[:LQ, 4 + j % 2, 0:C], cs[:, bass.ds(b, 1)], x_b, ALU.mult, ALU.add).then_inc(xacc_ready, 1)

            with dve.Fori(0, CHUNKS) as c:
                for m in range(IC):
                    shared_h(c, m)
                shared_acc(c)
            ps_flat = ps[:].rearrange("p k n -> p (k n)")

            def tile_in_T(t, par):
                dve.wait_ge(xsT_in_psum, t + 1)
                dve.tensor_copy(meta_in[:, par, :], xs[:, par, C:XW])
                dve.tensor_copy(xsT[:, par, :, :], ps[:, 6, 0:CC * T].rearrange("p (k q) -> p k q", k=CC)).then_inc(xsT_ready, 1)

            def routed(t, par):
                if tile_in(t, -1):
                    tile_in_T(t + 1, 1 - par)
                if tile_in(t):
                    dve.wait_ge(xsT_ready, t + 1)
                    if not isinstance(t, int) or t > 1:
                        dve.wait_ge(ry_ready, t - 1)
                    dve.tensor_copy(meta[:, par, :], meta_in[:, par, :])
                    dve.wait_ge(rsilu_ready, t + 1)
                    dve.tensor_tensor(h_rt[:, 0:IM], silu[:, 0:IM], ps_flat[:, IM:2 * IM], ALU.mult)
                    dve.tensor_tensor(h_rt[:, IM:I], silu[:, IM:I], ps_flat[:, 2 * IM + IR:W13], ALU.mult).then_inc(rh_ready, 1)
                if tile_in(t, 1):
                    o = 1 - par
                    dve.wait_ge(ry_in_psum, t)
                    if not isinstance(t, int) or t > 2:
                        dve.wait_ge(y_added[o], 8 * (t - 1 - o))
                    dve.tensor_scalar(idx_f[:, o, 0:1], meta[:, o, 1:2], 0.0, SKIP, ALU.is_equal, ALU.mult)
                    dve.tensor_scalar(y_out[:, o, :], ps[:, 5, 0:C], meta[:, o, 0:1], None, ALU.mult).then_inc(idx_ready, 1)
                    dve.wait_ge(idx_ready, t)
                    dve.scalar_tensor_tensor(idx[:, o:o + 1], meta[:, o, 1:2], -1.0, idx_f[:, o, 0:1], ALU.add, ALU.add).then_inc(ry_ready, 1)

            tile_in_T(0, 0)
            each_tile(dve, routed)


def lay_expert(w1, w2, w3):
    up = np.concatenate([w1[:IM], w3[:IM], w1[IM:], w3[IM:]]).T
    down = np.zeros((IC * 128, C), w2.dtype)
    down[:I] = w2.T
    return np.concatenate([up.reshape(CC, 128, W13).transpose(1, 0, 2).reshape(128, -1),
                           down.reshape(IC, 128, C).transpose(1, 0, 2).reshape(128, -1)], axis=1)


def kernel(**inputs):
    import numpy as _np
    import concourse.bacc as _bacc
    from concourse import mybir as _mybir
    from concourse.bass_utils import run_bass_kernel_spmd as _run
    nc = _bacc.Bacc("TRN2", target_bir_lowering=False, num_devices=1)
    a = {k: _np.asarray(v) for k, v in inputs.items()}
    yT = _np.zeros((CTX, B, LKA), a["ctx_768"].dtype)
    yT[:, :, :LKV] = a["ctx_768"].transpose(2, 0, 1)
    wkv = a["L0_xattn_Wkv"].reshape(CTX, 2, HD)
    arrays = {
        "x": a["x"],
        "ylay": _np.stack([yT[:128], _np.concatenate([yT[128:], yT[128:]])], axis=2),
        "wq": a["L0_xattn_Wq"],
        "wkv": _np.stack([wkv[:128], _np.concatenate([wkv[128:], wkv[128:]])], axis=2),
        "wproj": a["L0_xattn_Wproj"], "bproj": a["L0_xattn_bproj"],
        "eye": _np.eye(128, dtype=_np.float32),
        "router": a["L0_ffn_router_w"].T, "rbias": a["L0_ffn_routing_bias"],
        "experts": _np.stack([lay_expert(*(a[f"L0_ffn_sw{i}"] for i in (1, 2, 3)))]
                             + [lay_expert(*(a[f"L0_ffn_ew{i}"][e] for i in (1, 2, 3))) for e in range(E)]),
        "consts": constants(),
    }
    arrays = {k: _np.ascontiguousarray(v) for k, v in arrays.items()}
    args = [nc.dram_tensor(k, v.shape, _mybir.dt.from_np(v.dtype), kind="ExternalInput").ap() for k, v in arrays.items()]
    out = nc.dram_tensor("out", (B, LQ, C), F32, kind="ExternalOutput").ap()
    build(nc, *args, out)
    r = _run(nc, [arrays], core_ids=[0])
    return r.results[0]["out"]
```

```python
from contextlib import ExitStack

import numpy as np
import concourse.bass as bass
from concourse import mybir

F32 = mybir.dt.float32
F32R = mybir.dt.float32r
U32 = mybir.dt.uint32
I32 = mybir.dt.int32
ACT = mybir.ActivationFunctionType
ALU = mybir.AluOpType
AX = mybir.AxisListType

B, LQ, C = 16, 100, 256
LKV, CTX = 361, 192
H, DK = 16, 64
HD = H * DK
PAIRS = H // 2
STEPS = B * PAIRS
PER = 2 * PAIRS
CC = C // 128
LKE = LKV + 1
NKT = 3
KT = -(-LKV // NKT)
LKA = LKE + 2
SCALE = float(DK) ** -0.5
EPS = 1e-5
VU = 2 * NKT
HALF = HD // 2
GROUPS = ((0, 4), (4, B))
V_BANKS = (7, 0, 1)
KQ_BANKS = (6, 4, 2, 3)
Q_AT = 384
WARM_UP = 11

E, I = 7, 704
IC = 6
IM = (IC - 1) * 128
IR = I - IM
T = 128
NT = (B * LQ + E * (T - 1)) // T
NT_MIN = (B * LQ + T - 1) // T
ROUNDS = (NT + 1) // 2
ROUNDS_MIN = (NT_MIN - 1) // 2
NTX = 2 * ROUNDS + 2
W13 = 2 * I
WROW = CC * W13 + IC * C
XW = C + 2
CHB = 4
CHN = CHB * LQ
CHUNKS = B // CHB
SATURATED = 16.64
EARLY = 3
WITH_WEIGHTS = E - 2
WS_PARTS = 4
SKIP = 8192.0
PARTS = dict(tri=LQ, ones=LQ, desc=E, jt=NT_MIN, before=E * E, upto=E * E, tidx=NTX, ids=B)
CN = sum(PARTS.values())


def const_slice(cst, name):
    at = 0
    for k, n in PARTS.items():
        if k == name:
            return cst[:, at:at + n]
        at += n


def constants():
    q = np.arange(LQ)
    e = np.arange(E)
    row = dict(desc=E - e, jt=T * np.arange(NT_MIN), before=T * (e[None, :] < e[:, None]).reshape(-1),
               upto=(e[None, :] <= e[:, None]).reshape(-1), tidx=np.arange(NTX))
    full = {k: np.broadcast_to(v, (LQ, v.size)) for k, v in row.items()}
    full |= dict(tri=q[:, None] < q[None, :], ones=np.ones((LQ, LQ)), ids=q[:, None] + LQ * np.arange(B)[None, :] + 1)
    return np.concatenate([full[k].astype(np.float32) for k in PARTS], axis=1)


def build(nc, x, ylay, wq, wkv, wproj, bproj, eye, router, rbias, experts, consts, out):
    xs_dram = nc.dram_tensor("xs_dram", (NTX * T, XW), F32, kind="Internal").ap()
    with ExitStack() as ctx:
        def sb(name, shape, dt=F32):
            return ctx.enter_context(nc.sbuf_tensor(name, shape, dt))

        def sem(name):
            return ctx.enter_context(nc.semaphore(name))

        def sb_twice(name, shape, later):
            with ExitStack() as first:
                t = first.enter_context(nc.sbuf_tensor(name, shape, F32))
            t_later = ctx.enter_context(nc.sbuf_tensor(later, [128, CC * W13], F32R))
            ctx.enter_context(nc.sbuf_tensor(later + "_rest", [128, int(np.prod(shape[1:])) - CC * W13], F32))
            return t, t_later

        ident = sb("ident", [128, 128])
        x_sb, w_up_lo1 = sb_twice("x_sb", [LQ, B, C], "w_up_lo1")
        bp_sb = sb("bp_sb", [LQ, C])
        xnT, w_up_hi1 = sb_twice("xnT", [128, CC, B * LQ], "w_up_hi1")
        w_sh, w_up_hi0 = sb_twice("w_sh", [128, WROW], "w_up_hi0")
        expo = sb("expo", [LQ, B])
        stats = sb("stats", [LQ, B, 6])
        mv = sb("mv", [LQ, B, 2])
        stats_b = sb("stats_b", [LQ, 6])
        mv_b = sb("mv_b", [LQ, 2])
        rstd = sb("rstd", [LQ, B])
        router_sb = sb("router_sb", [128, CC, E])
        rb_sb = sb("rb_sb", [LQ, E])
        cst = sb("cst", [LQ, CN])
        logit = sb("logit", [LQ, B, E])
        attention = ctx.enter_context(ExitStack())

        taken = []

        def sb(name, shape, dt=F32):
            taken.append(int(np.prod(shape[1:])))
            return attention.enter_context(nc.sbuf_tensor(name, shape, dt))

        wq_sb = sb("wq_sb", [128, CC, HD])
        wp_raw = sb("wp_raw", [128, PAIRS, C])
        wp_hi = sb("wp_hi", [128, PAIRS, C], F32R)
        wp_lo = sb("wp_lo", [128, PAIRS, C], F32R)
        w_raw = w_sh[:, 0:4 * HD].rearrange("p (v a n) -> p v a n", v=2, a=2)
        y_raw = sb("y_raw", [128, 2, 2, LKA])
        ya_hi = sb("ya_hi", [128, 2, LKA], F32R)
        ya_lo = sb("ya_lo", [128, 2, LKA], F32R)
        yb_hl = sb("yb_hl", [128, 2, LKA], F32R)
        kT = sb("kT", [128, H, LKE], F32R)
        q_hi = sb("q_hi", [128, H, LQ], F32R)
        q_lo = sb("q_lo", [128, H, LQ], F32R)
        o_hi = sb("o_hi", [128, 2, LQ], F32R)
        o_lo = sb("o_lo", [128, 2, LQ], F32R)
        xn = sb("xn", [LQ, 2, C])
        sb("spare", [128, WITH_WEIGHTS * WROW - sum(taken)])
        w_hi_row = sb("w_hi", [128, WROW], F32R)
        w_lo_row = sb("w_lo", [128, WROW], F32R)
        w_hi, w_lo = (w[:, 0:4 * HD].rearrange("p (v a n) -> p v a n", v=2, a=2) for w in (w_hi_row, w_lo_row))
        v_sb = sb("v_sb", [KT, 2, NKT, HD])
        probs = sb("probs", [LQ, 2, 2, LKA])
        nmax = sb("nmax", [LQ, 2, 2])
        rsum = sb("rsum", [LQ, 2, 2])
        rinv = sb("rinv", [LQ, 2, 2])
        pT = sb("pT", [KT, 2, NKT, 2, LQ])
        x1T = sb("x1T", [128, CC, LQ])
        q_raw = sb("q_raw", [128, 2, 2, LQ])
        zeros = sb("zeros", [128, XW])
        one = sb("one", [128, 1])
        attention.close()

        shared = ctx.enter_context(ExitStack())

        def sb(name, shape, dt=F32):
            return shared.enter_context(nc.sbuf_tensor(name, shape, dt))

        sb("early_experts", [128, EARLY, WROW])
        x_hi = sb("x_hi", [128, CC, CHN], F32R)
        x_lo = sb("x_lo", [128, CC, CHN], F32R)
        h_hi = sb("h_hi", [128, IC, CHN], F32R)
        h_lo = sb("h_lo", [128, IC, CHN], F32R)
        h_raw = sb("h_raw", [128, 2, CHN])
        silu_c = sb("silu_c", [128, CHN])
        shared.close()

        def sb(name, shape, dt=F32):
            return ctx.enter_context(nc.sbuf_tensor(name, shape, dt))

        w_ex = sb("w_ex", [128, E, WROW])
        shapes = dict(key=[LQ, B, E], onehot=[LQ, B, E], cum=[LQ, 2, B, E], cmp=[LQ, E, max(NT_MIN, E, NTX)], tmp=[LQ, B, E])
        with ExitStack() as first:
            key, onehot, cum, cmp, tmp = (first.enter_context(nc.sbuf_tensor(n, shape, F32)) for n, shape in shapes.items())
        y_out = sb("y_out", [T, 2, C])
        sb("y_out_rest", [128, sum(int(np.prod(shape[1:])) for shape in shapes.values()) - 2 * C])
        small = sb("small", [LQ, 12, B])
        ntile = sb("ntile", [LQ, 4, E])
        pos = sb("pos", [LQ, B], U32)
        tile_ex = sb("tile_ex", [1, NTX], I32)
        tile_exf = sb("tile_exf", [1, NTX])
        tiles_used = sb("tiles_used", [1, 1], I32)
        xr, w_up_lo0 = sb_twice("xr", [LQ, B, XW], "w_up_lo0")
        w_up_hi, w_up_lo = (w_up_hi0, w_up_hi1), (w_up_lo0, w_up_lo1)
        hT = sb("hT", [128, IC, CHN])
        silu = sb("silu", [128, I])
        xs = sb("xs", [T, 2, XW])
        xsT_hi = sb("xsT_hi", [128, 2, CC, T], F32R)
        xsT_lo = sb("xsT_lo", [128, 2, CC, T], F32R)
        idx_f = sb("idx_f", [T, 2, 2])
        meta_in = sb("meta_in", [T, 2, 2])
        meta = sb("meta", [T, 2, 2])
        idx = sb("idx", [T, 2], U32)
        hT_flat = hT[:].rearrange("p m q -> p (m q)")
        h_rt = hT_flat[:, 0:I]
        hT_rt = [hT_flat[:, I + IC * T * i:I + IC * T * (i + 1)].rearrange("p (m q) -> p m q", m=IC) for i in range(2)]

        ps = ctx.enter_context(nc.psum_tensor("ps", [128, 8, 512], F32))
        ps_s, ps_t = ps[:, 0:2, :], ps[:, 2:4, :]
        ps_o, ps_y, ps_kq, ps_v = (ps[:, i, :] for i in range(4, 8))

        ld_id, ld_bp, ld_wq, ld_wp, ld_router, ld_wsh, ld_wex, ld_late, pads_ready, zero_ready, zero_done = (sem(n) for n in (
            "ld_id", "ld_bp", "ld_wq", "ld_wp", "ld_router", "ld_wsh", "ld_wex", "ld_late", "pads_ready", "zero_ready", "zero_done"))
        w_rounded, w_split, wp_hi_ready, wp_ready, wsh_hi_ready, wsh_ready = (sem(n) for n in (
            "w_rounded", "w_split", "wp_hi_ready", "wp_ready", "wsh_hi_ready", "wsh_ready"))
        y_step, y_split = (sem(n) for n in (
            "y_step", "y_split"))
        stat_ready, aggr_ready, rstd_ready, xn_ready, xt_ready, xnT_ready = (sem(n) for n in (
            "stat_ready", "aggr_ready", "rstd_ready", "xn_ready", "xt_ready", "xnT_ready"))
        kq_in_psum, kq_hi_ready, kq_lo_ready, q_hi_ready, q_ready = (sem(n) for n in (
            "kq_in_psum", "kq_hi_ready", "kq_lo_ready", "q_hi_ready", "q_ready"))
        v_in_psum, v_ready = (sem(n) for n in (
            "v_in_psum", "v_ready"))
        scores_ready, nmax_ready, exp_done, rinv_ready, p_ready, pT_in_psum, pT_ready = (sem(n) for n in (
            "scores_ready", "nmax_ready", "exp_done", "rinv_ready", "p_ready", "pT_in_psum", "pT_ready"))
        pv_ready, o_hi_ready, o_ready, proj_ready, bias_added, x1_ready = (sem(n) for n in (
            "pv_ready", "o_hi_ready", "o_ready", "proj_ready", "bias_added", "x1_ready"))
        stats1, aggr1, var1, x1n_ready, logits_in_psum, logit_ready = (sem(n) for n in (
            "stats1", "aggr1", "var1", "x1n_ready", "logits_in_psum", "logit_ready"))
        lmax_ready, prob_ready, onehot_ready, prefix_ready, tiles_known, pos_ready, dve_chain = (sem(n) for n in (
            "lmax_ready", "prob_ready", "onehot_ready", "prefix_ready", "tiles_known", "pos_ready", "dve_chain"))
        xr_step, xr_ready, xs_written = (sem(n) for n in (
            "xr_step", "xr_ready", "xs_written"))
        x_hi_ready, x_split, gu_in_psum, silu_ready, h_raw_ready, h_hi_ready, h_ready, down_ready, xacc_ready, base_stored = (sem(n) for n in (
            "x_hi_ready", "x_split", "gu_in_psum", "silu_ready", "h_raw_ready", "h_hi_ready", "h_ready", "down_ready", "xacc_ready", "base_stored"))
        xsT_in_psum, xsT_ready, rgu_in_psum, rsilu_ready, rh_ready, rhT_in_psum, rhT_ready, ry_in_psum, idx_ready, ry_ready = (sem(n) for n in (
            "xsT_in_psum", "xsT_ready", "rgu_in_psum", "rsilu_ready", "rh_ready", "rhT_in_psum", "rhT_ready", "ry_in_psum", "idx_ready", "ry_ready"))
        rw_hi_ready, rw_split, rw_split_last, xsT_hi_ready = (sem(n) for n in ("rw_hi_ready", "rw_split", "rw_split_last", "xsT_hi_ready"))
        ld_x = [sem(f"ld_x{i}") for i in range(4)]
        ld_wkv = [sem("ld_wk"), sem("ld_wv")]
        y_loaded, xs_loaded, y_added = ([sem(f"{n}{i}") for i in range(2)] for n in ("y_loaded", "xs_loaded", "y_added"))

        def tiles_in_use(eng):
            eng.wait_ge(tiles_known, 1)
            return eng.value_load(tiles_used[0:1, 0:1], min_val=NT_MIN, max_val=NT)

        def expert_of(eng, t):
            return eng.value_load(tile_ex[0:1, bass.ds(t, 1)], min_val=0, max_val=E - 1)

        def wait_late(eng, e):
            with eng.If(e > EARLY - 1):
                eng.wait_ge(ld_late, 16 * (E - EARLY))

        def up_part(e, k):
            return w_ex[:, bass.ds(e, 1), k * W13:(k + 1) * W13].rearrange("p o n -> p (o n)")

        def past(t, n):
            return not isinstance(t, int) or t > n

        def each_tile(eng, step, used):
            for t in range(3):
                step(t, t % 2)
            with eng.Fori(1, ROUNDS_MIN) as i:
                step(i * 2 + 1, 1)
                step(i * 2 + 2, 0)
            with eng.Fori(ROUNDS_MIN, ROUNDS) as i:
                for t, par in ((i * 2 + 1, 1), (i * 2 + 2, 0)):
                    with eng.If(used > t):
                        step(t, par)
                    with eng.If(used == t):
                        step(t, par, last=True)

        def each_chunk(eng, chunk, before_last=None):
            chunk(0, True)
            with eng.Fori(1, CHUNKS - 1) as c:
                chunk(c, True)
            if before_last:
                before_last()
            chunk(CHUNKS - 1, False)

        block = ctx.enter_context(nc.Block())

        def each_step(eng, step, after=None):
            for u in range(PER):
                step(0, u)
            with eng.Fori(1, B // 2 - 1) as it:
                for u in range(PER):
                    step(it, u)
            for u in range(PER + 3):
                step(B // 2 - 1, u)
                if after:
                    after(B // 2 - 1, u)

        def static(it):
            return isinstance(it, int)

        def steps_left(it, u, lag=0):
            return not static(it) or 0 <= it * PER + u - lag < STEPS

        @block.sync
        def _(sp):
            sp.dma_start(w_raw[:, 1], wkv[:, 1]).then_inc(ld_wkv[1], 16)
            sp.dma_start(w_raw[:, 0], wkv[:, 0]).then_inc(ld_wkv[0], 16)
            sp.dma_start(ident[:], eye).then_inc(ld_id, 16)
            sp.dma_start(wq_sb[:], wq.rearrange("(k p) n -> p k n", p=128)).then_inc(ld_wq, 16)
            for i in range(1, 4):
                sp.dma_start(x_sb[:, 4 * i:4 * i + 4, :], x.rearrange("b q c -> q b c")[:, 4 * i:4 * i + 4, :]).then_inc(ld_x[i], 16)
            sp.dma_start(y_raw[:, 1], ylay[:, 1]).then_inc(y_loaded[1], 16)
            sp.dma_start(bp_sb[:], bproj.partition_broadcast(LQ)).then_inc(ld_bp, 16)
            sp.dma_start(wp_raw[:], wproj.rearrange("(g p) n -> p g n", p=128)).then_inc(ld_wp, 16)
            sp.dma_start(router_sb[:], router.rearrange("(k p) e -> p k e", p=128)).then_inc(ld_router, 16)
            sp.dma_start(rb_sb[:], rbias.partition_broadcast(LQ)).then_inc(ld_router, 16)
            sp.dma_start(cst[:], consts).then_inc(ld_router, 16)
            sp.wait_ge(w_split, 3)
            sp.dma_start(w_sh[:], experts[0]).then_inc(ld_wsh, 16)
            sp.wait_ge(zero_ready, 1)
            sp.dma_start(xs_dram.rearrange("(t p) c -> p t c", p=T), zeros[:].unsqueeze(1).broadcast_to([T, NTX, XW])).then_inc(zero_done, 16)

            def load_y(b, par):
                sp.wait_ge(y_split, b - 1)
                sp.dma_start(y_raw[:, par], ylay[:, bass.ds(b, 1)].rearrange("p a k l -> p (a k) l")).then_inc(y_loaded[par], 16)

            with sp.Fori(1, B // 2) as it:
                for par in range(2):
                    load_y(2 * it + par, par)
            sp.wait_ge(x1_ready, B)
            for e in range(EARLY):
                sp.dma_start(w_ex[:, e, :], experts[e + 1]).then_inc(ld_wex, 16)

            def store_base(c):
                sp.wait_ge(xacc_ready, c * CHB + CHB)
                sp.dma_start(out.rearrange("b q c -> q b c")[:, bass.ds(c * CHB, CHB), :], x_sb[:, bass.ds(c * CHB, CHB), :]).then_inc(base_stored, 16)

            def load_tile(t, par):
                sp.dma_start(xs[:, par, :], xs_dram[bass.ds(t * T, T), :]).then_inc(xs_loaded[par], 16)

            def load_next(t, par):
                sp.wait_ge(xsT_ready, t)
                load_tile(t + 1, 1 - par)

            def load_late(lo, hi):
                for e in range(lo, hi):
                    sp.dma_start(w_ex[:, e, :], experts[e + 1]).then_inc(ld_late, 16)

            for c in range(CHUNKS):
                store_base(c)
                if c == 1:
                    sp.wait_ge(xs_written, 16 * B)
                    for t in range(2):
                        load_tile(t, t)
                if c == 2:
                    sp.wait_ge(xsT_ready, 1)
                    load_tile(2, 0)
            used = tiles_in_use(sp)
            load_late(EARLY, EARLY + 2)
            load_next(2, 0)
            e = expert_of(sp, 2)
            with sp.If(e < EARLY):
                load_next(3, 1)
                load_late(EARLY + 2, E)
            with sp.If(e > EARLY - 1):
                load_late(EARLY + 2, E)
                load_next(3, 1)
            load_next(4, 0)
            with sp.Fori(2, ROUNDS_MIN) as i:
                load_next(i * 2 + 1, 1)
                load_next(i * 2 + 2, 0)
            with sp.Fori(ROUNDS_MIN, ROUNDS) as i:
                for t, par in ((i * 2 + 1, 1), (i * 2 + 2, 0)):
                    with sp.If(used > t):
                        load_next(t, par)

        @block.gpsimd
        def _(pool):
            pool.memset(one[:], 1.0)
            pool.memset(probs[:, :, :, LKV:LKA], 0.0).then_inc(pads_ready, 1)
            pool.memset(zeros[:], 0.0).then_inc(zero_ready, 1)
            pool.wait_ge(zero_ready, 1)

            def split_y_part(i, b, par):
                if i == 0:
                    pool.wait_ge(y_loaded[par], 8 * (b - par) + 16)
                    pool.tensor_tensor(ya_hi[:, par, :], y_raw[:, par, 0, :], one[:].broadcast_to([128, LKA]), ALU.mult)
                if i == 1:
                    pool.tensor_tensor(yb_hl[:, par, :], y_raw[:, par, 1, :], one[:].broadcast_to([128, LKA]), ALU.mult).then_inc(y_step, 1)
                if i == 2:
                    pool.wait_ge(y_step, 2 * b + 1)
                    pool.tensor_tensor(ya_lo[:, par, :], y_raw[:, par, 0, :], ya_hi[:, par, :].bitcast(F32), ALU.subtract).then_inc(y_step, 1)
                if i == 3:
                    pool.wait_ge(y_step, 2 * b + 2)
                    pool.tensor_tensor(yb_hl[64:128, par, :], y_raw[64:128, par, 1, :], yb_hl[64:128, par, :].bitcast(F32), ALU.subtract).then_inc(y_split, 1)
                    pool.wait_ge(y_split, b + 1)

            def split_y(b, par):
                for i in range(4):
                    split_y_part(i, b, par)

            def deviations(i):
                lo, hi = GROUPS[i]
                pool.wait_ge(aggr_ready, 2 * i + 2)
                pool.tensor_tensor(rstd[:, lo:hi], rstd[:, lo:hi], expo[:, lo:hi], ALU.pow).then_inc(rstd_ready, 1)

            split_y(0, 0)
            deviations(0)
            split_y(1, 1)
            pool.wait_ge(ld_bp, 16)

            def row_of(b):
                return x_sb[:, bass.ds(b, 1), :].rearrange("p o c -> p (o c)")

            def split_q(n1, g):
                pair = slice(2 * g, 2 * g + 2)
                pool.wait_ge(kq_hi_ready, n1)
                pool.tensor_tensor(q_hi[:, pair, :], q_raw[:, g % 2], one[:].unsqueeze(2).broadcast_to([128, 2, LQ]), ALU.mult).then_inc(q_hi_ready, 1)
                pool.wait_ge(q_hi_ready, n1)
                pool.tensor_tensor(q_lo[:, pair, :], q_raw[:, g % 2], q_hi[:, pair, :].bitcast(F32), ALU.subtract).then_inc(q_ready, 1)

            for g in range(PAIRS - 1):
                split_q(g + 1, g)

            def step(it, u):
                n, buf = it * PER + u, u % 2
                b = it * 2 + u // PAIRS
                if not (static(it) and n > STEPS - PAIRS):
                    split_q(n + PAIRS, (u - 1) % PAIRS)
                if steps_left(it, u):
                    pool.wait_ge(rinv_ready, n + 1)
                    pool.tensor_tensor(probs[:, buf, :, 0:LKV], probs[:, buf, :, 0:LKV], rinv[:, buf, :].unsqueeze(2).broadcast_to([LQ, 2, LKV]), ALU.mult).then_inc(p_ready, 1)
                if 1 <= u % PAIRS < 5 and not (static(b) and b + 2 >= B):
                    if u % PAIRS == 1:
                        pool.wait_ge(kq_in_psum, PAIRS * b + PAIRS)
                    if u % PAIRS == 4:
                        pool.wait_ge(p_ready, n + 1)
                    split_y_part(u % PAIRS - 1, b + 2, u // PAIRS)
                if u % PAIRS == 6 and steps_left(it, u):
                    pool.wait_ge(xn_ready, b + 1)
                    pool.tensor_tensor(row_of(b), row_of(b), bp_sb[:], ALU.add).then_inc(bias_added, 1)
                if static(it) and it == 0 and u == 8:
                    deviations(1)
                if u % PAIRS == 5 and not (static(b) and b == 0):
                    pool.wait_ge(var1, b)
                    pool.tensor_tensor(rstd[:, bass.ds(b - 1, 1)], rstd[:, bass.ds(b - 1, 1)], expo[:, 0:1], ALU.pow).then_inc(rstd_ready, 1)

            each_step(pool, step)

            pool.wait_ge(var1, B)
            pool.tensor_tensor(rstd[:, B - 1:B], rstd[:, B - 1:B], expo[:, 0:1], ALU.pow).then_inc(rstd_ready, 1)
            pool.wait_ge(rstd_ready, B + 2)
            for c in range(CHUNKS):
                rows = slice(c * CHB, (c + 1) * CHB)
                pool.tensor_tensor(xr[:, rows, 0:C], x_sb[:, rows, :], mv[:, rows, 0:1].broadcast_to([LQ, CHB, C]), ALU.subtract).then_inc(xr_step, 1)
                pool.wait_ge(xr_step, c + 1)
                pool.tensor_tensor(xr[:, rows, 0:C], xr[:, rows, 0:C], rstd[:, rows].unsqueeze(2).broadcast_to([LQ, CHB, C]), ALU.mult).then_inc(xr_ready, 1)
            pool.wait_ge(xr_ready, CHUNKS)
            pool.wait_ge(zero_done, 16)
            pool.wait_ge(pos_ready, 1)
            for b in range(B):
                pool.indirect_dma_start(out=xs_dram, out_offset=bass.IndirectOffsetOnAxis(ap=pos[:, b:b + 1], axis=0),
                                        in_=xr[:, b, :], in_offset=None).then_inc(xs_written, 16)

            def add_tile(t):
                pool.wait_ge(ry_ready, t + 1)
                pool.indirect_dma_start(out=out.rearrange("b q c -> (b q) c"), out_offset=bass.IndirectOffsetOnAxis(ap=idx[:, t % 2:t % 2 + 1], axis=0),
                                        in_=y_out[:, t % 2, :], in_offset=None, bounds_check=B * LQ - 1, oob_is_err=False,
                                        compute_op=ALU.add).then_inc(y_added[t % 2], 16)

            def split_up(t):
                e = expert_of(pool, t)
                cols = slice((CC - 1) * W13, CC * W13)
                pool.wait_ge(rw_hi_ready, CC * t + CC)
                pool.tensor_tensor(w_up_lo[t % 2][:, cols], up_part(e, CC - 1), w_up_hi[t % 2][:, cols].bitcast(F32), ALU.subtract).then_inc(rw_split_last, 1)

            pool.wait_ge(xs_written, 16 * B)
            used = tiles_in_use(pool)
            split_up(0)
            pool.wait_ge(base_stored, 16 * CHUNKS)
            split_up(1)
            for t in range(1, NT_MIN):
                split_up(t + 1)
                add_tile(t - 1)
            for i in range(2):
                pool.wait_ge(y_added[i], 16 * ((NT_MIN - i) // 2))
            for t in range(NT_MIN, NT + 1):
                if t < NT:
                    with pool.If(used > t):
                        split_up(t + 1)
                with pool.If(used > t - 1):
                    add_tile(t - 1)
                    pool.wait_ge(y_added[(t - 1) % 2], 16 * ((t - 1) // 2 + 1))

        @block.tensor
        def _(pe):
            def project_kq(b, g, par, acc=ps_kq):
                cols = slice(g * 128, (g + 1) * 128)
                parts = ((w_lo, 0, ya_hi), (w_hi, 0, ya_lo), (w_lo, 1, yb_hl), (w_hi, 1, yb_hl), (w_hi, 0, ya_hi))
                for i, (w, a, y) in enumerate(parts):
                    pe.matmul(acc[:, 0:LKE], w[:, 0, a, cols], y[:, par, 0:LKE], start=i == 0, stop=i == 4)
                for k in range(CC):
                    last = pe.matmul(acc[:, Q_AT:Q_AT + LQ], wq_sb[:, k, cols], xnT[:, k, bass.ds(b * LQ, LQ)], start=k == 0, stop=k == CC - 1)
                last.then_inc(kq_in_psum, 1)

            def project_v(i, par, acc=ps_v):
                j, half = i % NKT, i // NKT
                rows, cols = slice(j * KT, (j + 1) * KT), slice(512 * half, 512 * half + 512)
                parts = ((ya_lo, w_hi, 0), (ya_hi, w_lo, 0), (yb_hl, w_lo, 1), (yb_hl, w_hi, 1), (ya_hi, w_hi, 0))
                for m, (y, w, a) in enumerate(parts):
                    last = pe.matmul(acc[:KT, :], y[:, par, rows], w[:, 1, a, cols], start=m == 0, stop=m == 4)
                last.then_inc(v_in_psum, 1)

            pe.wait_ge(zero_ready, 1)
            for i in range(WARM_UP):
                pe.matmul(ps[:, 2, 0:C], zeros[:, 0:128], zeros[:, 0:C], start=True, stop=True)
            pe.wait_ge(y_split, 1)
            for i in range(VU):
                if i % NKT == 0:
                    pe.wait_ge(w_split, i // NKT + 1)
                if i >= len(V_BANKS):
                    pe.wait_ge(v_ready, i - len(V_BANKS) + 1)
                project_v(i, 0, ps[:, V_BANKS[i % len(V_BANKS)], :])
            pe.wait_ge(ld_id, 16)
            pe.wait_ge(xn_ready, 2)
            for k in range(CC):
                for b in range(2):
                    last = pe.transpose(ps_y[:, (2 * k + b) * LQ:(2 * k + b + 1) * LQ], xn[:, b, k * 128:(k + 1) * 128], ident[:LQ, :LQ])
            last.then_inc(xt_ready, 2)
            pe.wait_ge(w_split, 3)
            pe.wait_ge(ld_wq, 16)
            pe.wait_ge(xnT_ready, 2)
            for g in range(PAIRS):
                if g >= len(KQ_BANKS):
                    pe.wait_ge(kq_lo_ready, g - len(KQ_BANKS) + 1)
                project_kq(0, g, 0, ps[:, KQ_BANKS[g % len(KQ_BANKS)], :])
            pe.wait_ge(v_ready, VU)

            def transpose_x(i):
                for k in range(CC):
                    last = pe.transpose(ps_v[:, (2 * k + i) * LQ:(2 * k + i + 1) * LQ], xn[:, i, k * 128:(k + 1) * 128], ident[:LQ, :LQ])
                return last

            def route():
                for k in range(CC):
                    last = pe.matmul(ps_v[:LQ, 0:E], x1T[:, k, :], router_sb[:, k, :], start=k == 0, stop=k == CC - 1)
                last.then_inc(logits_in_psum, 1)

            def step(it, u):
                n, buf, g = it * PER + u, u % 2, u % PAIRS
                b, par = it * 2 + u // PAIRS, (u // PAIRS) % 2
                more = not static(it) or b + 1 < B
                if steps_left(it, u):
                    if past(n, 0):
                        pe.wait_ge(exp_done, n)
                    if not more or not past(n, 0):
                        pe.wait_ge(kq_lo_ready, n + 1)
                    pe.wait_ge(q_ready, n + 1)
                    for h in range(2):
                        for m, qq in enumerate((q_lo, q_hi)):
                            last = pe.matmul(ps_s[:LQ, h, 0:LKE], qq[:, 2 * g + h, :], kT[:, 2 * g + h, :], start=m == 0, stop=m == 1)
                    last.then_inc(scores_ready, 1)
                if steps_left(it, u, 2):
                    gv, pv = (u - 2) % PAIRS, ((u - 2) // PAIRS) % 2
                    pe.wait_ge(pT_ready, n - 1)
                    if not (static(it) and n < 3):
                        pe.wait_ge(o_ready, n - 2)
                    if static(it) and n == 2:
                        pe.wait_ge(v_ready, VU)
                    elif gv == 0:
                        pe.wait_ge(v_ready, VU * (it * 2 + u // PAIRS) + VU)
                    for j in range(NKT):
                        last = pe.matmul(ps_o[:, 0:2 * LQ], v_sb[:, pv, j, gv * 128:(gv + 1) * 128], pT[:, buf, j, :, :], start=j == 0, stop=j == NKT - 1)
                    last.then_inc(pv_ready, 1)
                if steps_left(it, u, 3):
                    go = (u - 3) % PAIRS
                    pe.wait_ge(o_ready, n - 2)
                    if static(it) and n == 3:
                        pe.wait_ge(wp_ready, 2)
                    elif go == 0:
                        pe.wait_ge(x1_ready, it * 2 + (u - 3) // PAIRS)
                    for i, (o, w) in enumerate(((o_lo, wp_hi), (o_hi, wp_lo), (o_hi, wp_hi))):
                        last = pe.matmul(ps_y[:LQ, 0:C], o[:, 1 - buf, :], w[:, go, :], start=go == 0 and i == 0, stop=go == PAIRS - 1 and i == 2)
                    if go == PAIRS - 1:
                        last.then_inc(proj_ready, 1)
                if steps_left(it, u, 1):
                    pe.wait_ge(p_ready, n)
                    for h in range(2):
                        for j in range(NKT):
                            last = pe.transpose(ps_t[:KT, h, j * LQ:(j + 1) * LQ], probs[:, 1 - buf, h, j * KT:(j + 1) * KT], ident[:LQ, :LQ])
                    last.then_inc(pT_in_psum, 1)
                if g == 0 and not (static(b) and b < 2):
                    pe.wait_ge(xnT_ready, b + 2)
                    if static(b) and b == B:
                        pe.wait_ge(ld_router, 48)
                    route()
                if more and 1 <= g < 1 + VU:
                    pe.wait_ge(v_ready, VU * (b + 1) + g - 1)
                    if g == 1 and not (static(b) and b < 2):
                        pe.wait_ge(logit_ready, b - 1)
                    project_v(g - 1, 1 - par)
                if g == PAIRS - 1:
                    if more:
                        pe.wait_ge(v_ready, VU * (b + 2))
                    else:
                        pe.wait_ge(logit_ready, b - 1)
                    if not (static(b) and b + 2 >= B):
                        pe.wait_ge(xn_ready, b + 3)
                        last = transpose_x(0)
                    if not (static(b) and b == 0):
                        pe.wait_ge(x1n_ready, b)
                        last = transpose_x(1)
                    last.then_inc(xt_ready, 1)
                if more and steps_left(it, u):
                    if g == 0:
                        pe.wait_ge(y_split, b + 2)
                        pe.wait_ge(xnT_ready, b + 2)
                    pe.wait_ge(kq_lo_ready, n + PAIRS)
                    project_kq(b + 1, g, 1 - par)

            def shared_up(c, m):
                i = c * IC + m
                if m == 0:
                    pe.wait_ge(x_split, c + 1)
                if past(i, 1):
                    pe.wait_ge(h_raw_ready, i - 1)
                bank = 2 * (m % 2)
                for side in range(1 if m == IC - 1 else 2):
                    lo = 2 * IM if m == IC - 1 else side * IM + m * 128
                    parts = [(w, xx, k) for w, xx in ((w_lo_row, x_hi), (w_hi_row, x_lo), (w_hi_row, x_hi)) for k in range(CC)]
                    for j, (w, xx, k) in enumerate(parts):
                        last = pe.matmul(ps[:, bank + side, 0:CHN], w[:, k * W13 + lo:k * W13 + lo + 128], xx[:, k, :], start=j == 0, stop=j == len(parts) - 1)
                last.then_inc(gu_in_psum, 1)

            def after(it, u):
                if u == PER:
                    pe.wait_ge(wsh_ready, WS_PARTS)
                    shared_up(0, 0)

            each_step(pe, step, after)

            shared_up(0, 1)
            pe.wait_ge(logit_ready, B - 1)
            pe.wait_ge(x1n_ready, B)
            transpose_x(1).then_inc(xt_ready, 1)
            shared_up(0, 2)
            pe.wait_ge(xnT_ready, B + 3)
            route()

            def shared_down(c):
                for j in range(CHB):
                    if past(c, 0) or j > 1:
                        pe.wait_ge(xacc_ready, c * CHB + j - 1)
                    parts = [(h, w, m) for m in range(IC) for h, w in ((h_lo, w_hi_row), (h_hi, w_lo_row), (h_hi, w_hi_row))]
                    for i, (h, w, m) in enumerate(parts):
                        rows = 128 if m < IC - 1 else IR
                        if j == 0 and i % 3 == 0:
                            pe.wait_ge(h_ready, c * IC + m + 1)
                        last = pe.matmul(ps[:LQ, 4 + j % 2, 0:C], h[:rows, m, j * LQ:(j + 1) * LQ],
                                         w[:rows, CC * W13 + m * C:CC * W13 + (m + 1) * C], start=i == 0, stop=i == len(parts) - 1)
                    last.then_inc(down_ready, 1)

            def shared_chunk(c, more):
                first = not past(c, 0)
                for m in range(3 if first else 0, IC):
                    if first and m == 4:
                        pe.wait_ge(onehot_ready, 1)
                        pe.wait_ge(logit_ready, B)
                        for to, part in ((0, "tri"), (128, "ones")):
                            last = pe.matmul(ps[:LQ, 7, to:to + B * E], const_slice(cst, part), onehot[:].rearrange("p b e -> p (b e)"), start=True, stop=True)
                        last.then_inc(prefix_ready, 1)
                    shared_up(c, m)
                shared_down(c)

            def transpose_tile(t, par):
                pe.wait_ge(xs_loaded[par], 8 * (t - par) + 16)
                for k in range(CC):
                    last = pe.transpose(ps[:, 6, k * T:(k + 1) * T], xs[:, par, k * 128:(k + 1) * 128], ident[:])
                last.then_inc(xsT_in_psum, 1)

            each_chunk(pe, shared_chunk, lambda: transpose_tile(0, 0))
            used = tiles_in_use(pe)
            pe.wait_ge(ld_wex, 16 * EARLY)
            pe.wait_ge(xacc_ready, B)

            def routed(t, par, last=False):
                if not last:
                    transpose_tile(t + 1, 1 - par)
                    if past(t, 0):
                        pe.wait_ge(rh_ready, t)
                    pe.wait_ge(xsT_ready, t + 1)
                    for lo in range(0, W13, 512):
                        n = min(512, W13 - lo)
                        parts = [(xx, w, k) for xx, w in ((xsT_hi, w_up_lo), (xsT_lo, w_up_hi), (xsT_hi, w_up_hi)) for k in range(CC)]
                        for i, (xx, w, k) in enumerate(parts):
                            if lo == 0 and i < CC:
                                pe.wait_ge((rw_split, rw_split_last)[k], t + 1)
                            mm = pe.matmul(ps[:, lo // 512, lo % 512:lo % 512 + n], xx[:, par, k, :], w[par][:, k * W13 + lo:k * W13 + lo + n], start=i == 0, stop=i == len(parts) - 1)
                    mm.then_inc(rgu_in_psum, 1)
                if past(t, 0):
                    e = expert_of(pe, t - 1)
                    wait_late(pe, e)
                    pe.wait_ge(rhT_ready, t)
                    if past(t, 1):
                        pe.wait_ge(ry_ready, t - 1)
                    for m in range(IC):
                        rows = 128 if m < IC - 1 else IR
                        mm = pe.matmul(ps[:, 5, 0:C], hT_rt[1 - par][:rows, m, :],
                                       w_ex[:rows, bass.ds(e, 1), CC * W13 + m * C:CC * W13 + (m + 1) * C].rearrange("p o n -> p (o n)"), start=m == 0, stop=m == IC - 1)
                    mm.then_inc(ry_in_psum, 1)
                if not last:
                    pe.wait_ge(rh_ready, t + 1)
                    for m in range(IC):
                        cols = 128 if m < IC - 1 else IR
                        mm = pe.transpose(ps[:cols, 3 + m // 4, (m % 4) * T:(m % 4 + 1) * T], h_rt[:, m * 128:m * 128 + cols], ident[:])
                    mm.then_inc(rhT_in_psum, 1)

            each_tile(pe, routed, used)

        @block.scalar
        def _(act):
            act.dma_start(y_raw[:, 0], ylay[:, 0]).then_inc(y_loaded[0], 16)
            act.dma_start(x_sb[:, 0:4, :], x.rearrange("b q c -> q b c")[:, 0:4, :]).then_inc(ld_x[0], 16)
            act.wait_ge(ld_wkv[1], 16)
            for half in range(2):
                cols = slice(512 * half, 512 * half + 512)
                act.activation(w_hi[:, 1, :, cols], w_raw[:, 1, :, cols], ACT.Copy).then_inc(w_rounded, 1)
            act.wait_ge(ld_wkv[0], 16)
            act.activation(w_hi[:, 0], w_raw[:, 0], ACT.Copy).then_inc(w_rounded, 1)

            def kq_hi(n1, g, acc=ps_kq):
                act.wait_ge(kq_in_psum, n1)
                for h in range(2):
                    act.activation(kT[0:64, 2 * g + h, :], acc[64 * h:64 * h + 64, 0:LKE], ACT.Copy)
                if not (isinstance(n1, int) and n1 < 3):
                    act.wait_ge(q_ready, n1 - 2)
                for h in range(2):
                    for half in range(2):
                        last = act.activation(q_raw[64 * half:64 * half + 64, g % 2, h, :], acc[64 * h:64 * h + 64, Q_AT:Q_AT + LQ], ACT.Copy, scale=SCALE)
                last.then_inc(kq_hi_ready, 1)

            def v_copy(n1, i, par, acc=ps_v):
                act.wait_ge(v_in_psum, n1)
                act.activation(v_sb[:, par, i % NKT, 512 * (i // NKT):512 * (i // NKT) + 512], acc[:KT, :], ACT.Copy).then_inc(v_ready, 1)

            for i in range(VU):
                v_copy(i + 1, i, 0, ps[:, V_BANKS[i % len(V_BANKS)], :])
            act.wait_ge(xt_ready, 2)
            act.activation(xnT[:, :, 0:2 * LQ], ps_y[:, 0:4 * LQ].rearrange("p (k q) -> p k q", k=CC), ACT.Copy).then_inc(xnT_ready, 2)
            for g in range(PAIRS):
                kq_hi(g + 1, g, ps[:, KQ_BANKS[g % len(KQ_BANKS)], :])

            def copy_xT(i, b):
                x_t = ps_v[:, 0:4 * LQ].rearrange("p (k i q) -> p k i q", k=CC, i=2)[:, :, i, :]
                if i == 1:
                    act.activation(x1T[:], x_t, ACT.Copy)
                return act.activation(xnT[:, :, bass.ds(b * LQ, LQ)], x_t, ACT.Copy)

            def step(it, u):
                n, buf, g = it * PER + u, u % 2, u % PAIRS
                b, par = it * 2 + u // PAIRS, (u // PAIRS) % 2
                more = not static(it) or b + 1 < B
                if steps_left(it, u):
                    act.wait_ge(nmax_ready, n + 1)
                    for h in range(2):
                        last = act.activation(probs[:, buf, h, 0:LKV], ps_s[:LQ, h, 0:LKV], ACT.Exp, bias=nmax[:, buf, h:h + 1], scale=1.0, accum_out=rsum[:, buf, h:h + 1])
                    last.then_inc(exp_done, 1)
                if steps_left(it, u, 2):
                    act.wait_ge(pv_ready, n - 1)
                    for h in range(2):
                        last = act.activation(o_hi[64 * h:64 * h + 64, buf, :], ps_o[64 * h:64 * h + 64, h * LQ:(h + 1) * LQ], ACT.Copy)
                    last.then_inc(o_hi_ready, 1)
                if more and 1 <= g < 1 + VU:
                    v_copy(VU * (b + 1) + g, g - 1, 1 - par)
                if more and steps_left(it, u):
                    kq_hi(n + PAIRS + 1, g)
                if static(it) and 1 + STEPS - PAIRS <= n < 1 + STEPS - PAIRS + WS_PARTS:
                    i = n - 1 - (STEPS - PAIRS)
                    cols = slice(i * WROW // WS_PARTS, (i + 1) * WROW // WS_PARTS)
                    act.wait_ge(ld_wsh, 16)
                    act.activation(w_hi_row[:, cols], w_sh[:, cols], ACT.Copy).then_inc(wsh_hi_ready, 1)
                if static(it) and it == 0 and u < 2:
                    act.wait_ge(ld_wp, 16)
                    act.activation(wp_hi[:, 4 * u:4 * u + 4], wp_raw[:, 4 * u:4 * u + 4], ACT.Copy).then_inc(wp_hi_ready, 1)
                if g == PAIRS - 1:
                    act.wait_ge(xt_ready, b + 3)
                    if not (static(b) and b + 2 >= B):
                        last = copy_xT(0, b + 2)
                    if not (static(b) and b == 0):
                        last = copy_xT(1, b - 1)
                    last.then_inc(xnT_ready, 1)

            def split_x(c):
                act.activation(x_hi[:], xnT[:, :, bass.ds(c * CHN, CHN)], ACT.Copy).then_inc(x_hi_ready, 1)

            def after(it, u):
                if u == PER - 1:
                    split_x(0)

            each_step(act, step, after)

            def shared_h(c, m):
                i = c * IC + m
                rows = 128 if m < IC - 1 else IR
                act.wait_ge(gu_in_psum, i + 1)
                if past(i, 0):
                    act.wait_ge(h_raw_ready, i)
                act.activation(silu_c[:rows], ps[:rows, 2 * (m % 2), 0:CHN], ACT.Silu).then_inc(silu_ready, 1)
                act.wait_ge(h_raw_ready, i + 1)
                act.activation(h_hi[:rows, m, :], h_raw[:rows, m % 2], ACT.Copy).then_inc(h_hi_ready, 1)

            shared_h(0, 0)
            shared_h(0, 1)
            act.wait_ge(xt_ready, B + 3)
            copy_xT(1, B - 1).then_inc(xnT_ready, 1)
            shared_h(0, 2)
            act.wait_ge(lmax_ready, 1)
            act.activation(small[:, 1, :], small[:, 0, :], ACT.Exp, scale=-1.0).then_inc(prob_ready, 1)

            def shared_chunk(c, more):
                for m in range(0 if past(c, 0) else 3, IC):
                    shared_h(c, m)
                if more:
                    split_x(c + 1)

            def split_up(e, par):
                for k in range(CC):
                    act.activation(w_up_hi[par][:, k * W13:(k + 1) * W13], up_part(e, k), ACT.Copy).then_inc(rw_hi_ready, 1)

            def split_first():
                act.wait_ge(tiles_known, 1)
                act.wait_ge(ld_wex, 16 * EARLY)
                e = expert_of(act, 0)
                with act.If(e < EARLY):
                    split_up(e, 0)

            each_chunk(act, shared_chunk, split_first)
            used = tiles_in_use(act)
            ps_flat = ps[:].rearrange("p k n -> p (k n)")

            def routed(t, par, last=False):
                if past(t, 0):
                    act.wait_ge(rhT_in_psum, t)
                    hT_ps = ps_flat[:, 3 * 512:3 * 512 + IC * T].rearrange("p (m q) -> p m q", m=IC)
                    act.activation(hT_rt[1 - par][:, 0:IC - 1, :], hT_ps[:, 0:IC - 1, :], ACT.Copy)
                    act.activation(hT_rt[1 - par][:IR, IC - 1, :], hT_ps[:IR, IC - 1, :], ACT.Copy).then_inc(rhT_ready, 1)
                if last:
                    return
                if past(t, 0):
                    act.wait_ge(rgu_in_psum, t)
                else:
                    e = expert_of(act, 0)
                    with act.If(e > EARLY - 1):
                        act.wait_ge(ld_late, 16 * (E - EARLY))
                        split_up(e, 0)
                e = expert_of(act, t + 1)
                wait_late(act, e)
                split_up(e, 1 - par)
                act.wait_ge(rgu_in_psum, t + 1)
                if past(t, 0):
                    act.wait_ge(rh_ready, t)
                act.activation(silu[:, 0:IM], ps_flat[:, 0:IM], ACT.Silu)
                act.activation(silu[:, IM:I], ps_flat[:, 2 * IM:2 * IM + IR], ACT.Silu).then_inc(rsilu_ready, 1)

            each_tile(act, routed, used)

        @block.vector
        def _(dve):
            dve.memset(expo[:], -0.5)
            for half in range(2):
                cols = slice(512 * half, 512 * half + 512)
                dve.wait_ge(w_rounded, half + 1)
                dve.tensor_tensor(w_lo[:, 1, :, cols], w_raw[:, 1, :, cols], w_hi[:, 1, :, cols].bitcast(F32), ALU.subtract).then_inc(w_split, 1)

            def moments(lo, hi):
                for b in range(lo, hi):
                    last = dve.bn_stats(stats[:, b, :], x_sb[:, b, :])
                last.then_inc(stat_ready, 1)

            def variance(i):
                lo, hi = GROUPS[i]
                for b in range(lo, hi):
                    last = dve.bn_aggr(mv[:, b, :], stats[:, b, :])
                last.then_inc(aggr_ready, 1)
                dve.wait_ge(aggr_ready, 2 * i + 1)
                dve.tensor_scalar(rstd[:, lo:hi], mv[:, lo:hi, 1], EPS, None, ALU.add).then_inc(aggr_ready, 1)

            def row_of(b):
                return x_sb[:, bass.ds(b, 1), :].rearrange("p o c -> p (o c)")

            def normalise(b, i, ready):
                mean = mv[:, bass.ds(b, 1), 0:1].rearrange("p o s -> p (o s)")
                dve.tensor_scalar(xn[:, i, :], row_of(b), mean, rstd[:, bass.ds(b, 1)], ALU.subtract, ALU.mult).then_inc(ready, 1)

            dve.wait_ge(ld_x[0], 16)
            moments(0, 4)
            dve.wait_ge(stat_ready, 1)
            variance(0)
            dve.wait_ge(w_rounded, 3)
            dve.tensor_tensor(w_lo[:, 0], w_raw[:, 0], w_hi[:, 0].bitcast(F32), ALU.subtract).then_inc(w_split, 1)
            dve.wait_ge(rstd_ready, 1)
            for b in range(2):
                normalise(b, b, xn_ready)

            def kq_lo(n1, g, acc=ps_kq):
                dve.wait_ge(kq_hi_ready, n1)
                for h in range(2):
                    last = dve.tensor_tensor(kT[64:128, 2 * g + h, :], acc[64 * h:64 * h + 64, 0:LKE], kT[0:64, 2 * g + h, :].bitcast(F32), ALU.subtract)
                last.then_inc(kq_lo_ready, 1)

            for g in range(PAIRS):
                kq_lo(g + 1, g, ps[:, KQ_BANKS[g % len(KQ_BANKS)], :])
            dve.wait_ge(pads_ready, 1)
            dve.wait_ge(ld_router, 48)

            def x1_stats(b):
                dve.bn_stats(stats_b[:], row_of(b)).then_inc(stats1, 1)

            def x1_moments():
                dve.bn_aggr(mv_b[:], stats_b[:]).then_inc(aggr1, 1)

            def x1_variance(b):
                dve.wait_ge(aggr1, b + 1)
                dve.tensor_copy(mv[:, bass.ds(b, 1), 0:1].rearrange("p o s -> p (o s)"), mv_b[:, 0:1])
                dve.tensor_scalar(rstd[:, bass.ds(b, 1)], mv_b[:, 1:2], EPS, None, ALU.add).then_inc(var1, 1)

            def take_logits(b):
                dve.wait_ge(logits_in_psum, b + 1)
                dve.tensor_tensor(logit[:, bass.ds(b, 1), :].rearrange("p o e -> p (o e)"), ps_v[:LQ, 0:E], rb_sb[:], ALU.add).then_inc(logit_ready, 1)

            def step(it, u):
                n, buf, g = it * PER + u, u % 2, u % PAIRS
                b = it * 2 + u // PAIRS
                if steps_left(it, u):
                    dve.wait_ge(scores_ready, n + 1)
                    dve.tensor_reduce(nmax[:, buf, :], ps_s[:LQ, :, 0:LKV], AX.X, ALU.max, negate=True).then_inc(nmax_ready, 1)
                if past(n, 0) and not (static(it) and n > STEPS - PAIRS):
                    kq_lo(n + PAIRS, (u - 1) % PAIRS)
                if steps_left(it, u):
                    dve.wait_ge(exp_done, n + 1)
                    dve.reciprocal(rinv[:, buf, :], rsum[:, buf, :]).then_inc(rinv_ready, 1)
                bo = b - 1
                if not (static(b) and b == 0):
                    if g == 3:
                        dve.wait_ge(x1_ready, b)
                    if g == 4:
                        dve.wait_ge(stats1, b)
                if steps_left(it, u, 1):
                    dve.wait_ge(pT_in_psum, n)
                    dve.tensor_copy(pT[:, 1 - buf, :, :, :].rearrange("p j h q -> p h j q"), ps_t[:KT, :, 0:NKT * LQ].rearrange("p h (j q) -> p h j q", j=NKT)).then_inc(pT_ready, 1)
                if steps_left(it, u, 2):
                    dve.wait_ge(o_hi_ready, n - 1)
                    for h in range(2):
                        rows = slice(64 * h, 64 * h + 64)
                        last = dve.tensor_tensor(o_lo[rows, buf, :], ps_o[rows, h * LQ:(h + 1) * LQ], o_hi[rows, buf, :].bitcast(F32), ALU.subtract)
                    last.then_inc(o_ready, 1)
                if not (static(b) and b == 0):
                    if g == 2:
                        dve.wait_ge(proj_ready, b)
                        dve.wait_ge(bias_added, b)
                        dve.tensor_tensor(row_of(bo), row_of(bo), ps_y[:LQ, 0:C], ALU.add).then_inc(x1_ready, 1)
                    if g == 3:
                        x1_stats(bo)
                    if g == 4:
                        x1_moments()
                    if g == 5:
                        x1_variance(bo)
                if static(it) and 1 + STEPS - PAIRS <= n < 1 + STEPS - PAIRS + WS_PARTS:
                    i = n - 1 - (STEPS - PAIRS)
                    cols = slice(i * WROW // WS_PARTS, (i + 1) * WROW // WS_PARTS)
                    dve.wait_ge(wsh_hi_ready, i + 1)
                    dve.tensor_tensor(w_lo_row[:, cols], w_sh[:, cols], w_hi_row[:, cols].bitcast(F32), ALU.subtract).then_inc(wsh_ready, 1)
                if static(it) and it == 0 and 4 <= u < 7:
                    dve.wait_ge(ld_x[u - 3], 16)
                    moments(4 * u - 12, 4 * u - 8)
                if static(it) and it == 0 and u == 7:
                    dve.wait_ge(stat_ready, 4)
                    variance(1)
                if static(it) and it == 0 and 1 <= u < 3:
                    groups = slice(4 * u - 4, 4 * u)
                    dve.wait_ge(wp_hi_ready, u)
                    dve.tensor_tensor(wp_lo[:, groups], wp_raw[:, groups], wp_hi[:, groups].bitcast(F32), ALU.subtract).then_inc(wp_ready, 1)
                if g == 6:
                    if static(it) and b == 1:
                        dve.wait_ge(rstd_ready, 3)
                    if not (static(b) and b + 2 >= B):
                        dve.wait_ge(xt_ready, b + 2)
                        normalise(b + 2, 0, xn_ready)
                    if not (static(b) and b == 0):
                        dve.wait_ge(rstd_ready, b + 2)
                        dve.wait_ge(xt_ready, b + 2)
                        normalise(bo, 1, x1n_ready)
                if g == 0 and not (static(b) and b < 2):
                    take_logits(b - 2)

            def split_x(c):
                dve.wait_ge(x_hi_ready, c + 1)
                dve.tensor_tensor(x_lo[:], xnT[:, :, bass.ds(c * CHN, CHN)], x_hi[:].bitcast(F32), ALU.subtract).then_inc(x_split, 1)

            def shared_h(c, m):
                i = c * IC + m
                rows = 128 if m < IC - 1 else IR
                up = ps[:, 2 * (m % 2) + 1, 0:CHN] if m < IC - 1 else ps[IR:128, 2 * (m % 2), 0:CHN]
                dve.wait_ge(silu_ready, i + 1)
                dve.tensor_tensor(h_raw[:rows, m % 2], silu_c[:rows], up, ALU.mult).then_inc(h_raw_ready, 1)
                dve.wait_ge(h_hi_ready, i + 1)
                dve.tensor_tensor(h_lo[:rows, m, :], h_raw[:rows, m % 2], h_hi[:rows, m, :].bitcast(F32), ALU.subtract).then_inc(h_ready, 1)

            def after(it, u):
                if u == PER - 1:
                    split_x(0)

            each_step(dve, step, after)

            def link(ins):
                chain[0] += 1
                ins.then_inc(dve_chain, 1)
                dve.wait_ge(dve_chain, chain[0])

            chain = [0]
            last_b = B - 1
            dve.wait_ge(x1_ready, B)
            x1_stats(last_b)
            dve.wait_ge(stats1, B)
            x1_moments()
            x1_variance(last_b)

            shared_h(0, 0)
            dve.wait_ge(rstd_ready, B + 2)
            dve.wait_ge(xt_ready, B + 2)
            normalise(last_b, 1, x1n_ready)
            shared_h(0, 1)
            shared_h(0, 2)
            take_logits(last_b)

            def over_e(v):
                return v.unsqueeze(2).broadcast_to([LQ, B, E])

            def over_b(v):
                return v.unsqueeze(1).broadcast_to([LQ, B, E])

            lmax, ex, kmax, dmax, prob, tw, cs, pos_f = (small[:, i, :] for i in range(8))
            desc = const_slice(cst, "desc")

            def shared_acc(c, more):
                if not past(c, 0):
                    dve.wait_ge(xr_ready, 1)
                for j in range(CHB):
                    b = c * CHB + j
                    dve.wait_ge(down_ready, b + 1)
                    dve.scalar_tensor_tensor(row_of(b), ps[:LQ, 4 + j % 2, 0:C], cs[:, bass.ds(b, 1)], row_of(b), ALU.mult, ALU.add).then_inc(xacc_ready, 1)
                    if j == 0 and more:
                        split_x(c + 1)

            dve.wait_ge(logit_ready, B)
            link(dve.tensor_scalar(logit[:], logit[:], 50.0, -50.0, ALU.min, ALU.max))
            dve.tensor_reduce(lmax, logit[:], AX.X, ALU.max).then_inc(lmax_ready, 1)
            dve.wait_ge(lmax_ready, 1)
            dve.tensor_scalar(key[:], logit[:], SATURATED, None, ALU.min)
            link(dve.tensor_scalar(kmax, lmax, SATURATED, None, ALU.min))
            link(dve.tensor_tensor(tmp[:], key[:], over_e(kmax), ALU.is_equal))
            link(dve.tensor_tensor(tmp[:], tmp[:], over_b(desc), ALU.mult))
            link(dve.tensor_reduce(dmax, tmp[:], AX.X, ALU.max))
            dve.tensor_tensor(onehot[:], over_b(desc), over_e(dmax), ALU.is_equal).then_inc(onehot_ready, 1)
            shared_h(0, 3)
            dve.wait_ge(prob_ready, 1)
            link(dve.tensor_scalar(ex, ex, 1.0, None, ALU.add))
            link(dve.reciprocal(prob, ex))
            link(dve.tensor_scalar(prob, prob, 1e-8, 1.0, ALU.max, ALU.min))
            link(dve.tensor_scalar(tw, prob, 0.5, 1e-8, ALU.add, ALU.add))
            link(dve.tensor_scalar(tw, tw, 0.5, 2.0, ALU.max, ALU.min))
            link(dve.reciprocal(tw, tw))
            link(dve.tensor_scalar(cs, tw, 0.5, None, ALU.mult))
            link(dve.tensor_tensor(xr[:, :, C], prob, tw, ALU.mult))
            link(dve.tensor_copy(xr[:, :, C + 1], const_slice(cst, "ids")))
            shared_h(0, 4)
            shared_h(0, 5)
            dve.wait_ge(prefix_ready, 1)
            before = ps[:LQ, 7, 0:B * E].rearrange("p (b e) -> p b e", b=B)
            count = ps[:LQ, 7, 128:128 + B * E].rearrange("p (b e) -> p b e", b=B)
            link(dve.tensor_copy(cum[:, 0], count))
            side, s = 0, 1
            while s < B:
                dve.tensor_copy(cum[:, 1 - side, 0:s, :], cum[:, side, 0:s, :])
                link(dve.tensor_tensor(cum[:, 1 - side, s:B, :], cum[:, side, s:B, :], cum[:, side, 0:B - s, :], ALU.add))
                side, s = 1 - side, 2 * s
            upto, ranks = cum[:, side], cum[:, 1 - side]
            tiles, start_row, end_tile = (ntile[:, i, :] for i in range(3))
            link(dve.tensor_tensor(cmp[:, :, 0:NT_MIN], upto[:, B - 1, :].unsqueeze(2).broadcast_to([LQ, E, NT_MIN]),
                                   const_slice(cst, "jt").unsqueeze(1).broadcast_to([LQ, E, NT_MIN]), ALU.is_gt))
            link(dve.tensor_reduce(tiles, cmp[:, :, 0:NT_MIN], AX.X, ALU.add))
            for name, to in (("before", start_row), ("upto", end_tile)):
                link(dve.tensor_tensor(cmp[:, :, 0:E], const_slice(cst, name).rearrange("p (a b) -> p a b", a=E),
                                       tiles.unsqueeze(1).broadcast_to([LQ, E, E]), ALU.mult))
                link(dve.tensor_reduce(to, cmp[:, :, 0:E], AX.X, ALU.add))
            shared_acc(0, True)
            over = cmp[:].rearrange("p a b -> p (a b)")[0:1, 0:NTX * E].rearrange("p (t e) -> p t e", t=NTX)
            link(dve.tensor_tensor(over, end_tile[0:1].unsqueeze(1).broadcast_to([1, NTX, E]),
                                   const_slice(cst, "tidx")[0:1].unsqueeze(2).broadcast_to([1, NTX, E]), ALU.is_le))
            link(dve.tensor_reduce(tile_exf[:], over, AX.X, ALU.add))
            dve.tensor_scalar(tile_ex[:], tile_exf[:], float(E - 1), None, ALU.min)
            dve.tensor_copy(tiles_used[:], end_tile[0:1, E - 1:E]).then_inc(tiles_known, 1)
            link(dve.tensor_tensor(ranks, upto, before, ALU.add))
            link(dve.tensor_tensor(ranks, ranks, count, ALU.subtract))
            link(dve.tensor_tensor(ranks, ranks, over_b(start_row), ALU.add))
            link(dve.tensor_tensor(ranks, ranks, onehot[:], ALU.mult))
            link(dve.tensor_reduce(pos_f, ranks, AX.X, ALU.add))
            dve.tensor_copy(pos[:], pos_f).then_inc(pos_ready, 1)
            dve.wait_ge(xr_ready, CHUNKS)

            def shared_chunk(c, more):
                for m in range(IC):
                    shared_h(c, m)
                shared_acc(c, more)

            def tile_in_T(t, par):
                dve.wait_ge(xsT_in_psum, t + 1)
                dve.tensor_copy(meta_in[:, par, :], xs[:, par, C:XW])
                x_t = ps[:, 6, 0:CC * T].rearrange("p (k q) -> p k q", k=CC)
                dve.tensor_copy(xsT_hi[:, par, :, :], x_t).then_inc(xsT_hi_ready, 1)
                dve.wait_ge(xsT_hi_ready, t + 1)
                dve.tensor_tensor(xsT_lo[:, par, :, :], x_t, xsT_hi[:, par, :, :].bitcast(F32), ALU.subtract).then_inc(xsT_ready, 1)

            def split_up(t, e, par):
                dve.wait_ge(rw_hi_ready, CC * t + 1)
                dve.tensor_tensor(w_up_lo[par][:, 0:W13], up_part(e, 0), w_up_hi[par][:, 0:W13].bitcast(F32), ALU.subtract).then_inc(rw_split, 1)

            with dve.Fori(1, CHUNKS - 1) as c:
                shared_chunk(c, True)
            tile_in_T(0, 0)
            dve.wait_ge(xs_written, 16 * B)
            e = expert_of(dve, 0)
            with dve.If(e < EARLY):
                split_up(0, e, 0)
            shared_chunk(CHUNKS - 1, False)
            ps_flat = ps[:].rearrange("p k n -> p (k n)")

            def finish(t, par):
                o = 1 - par
                dve.wait_ge(ry_in_psum, t)
                if past(t, 2):
                    dve.wait_ge(y_added[o], 8 * (t - 1 - o))
                dve.tensor_scalar(idx_f[:, o, 0:1], meta[:, o, 1:2], 0.0, SKIP, ALU.is_equal, ALU.mult)
                dve.tensor_scalar(y_out[:, o, :], ps[:, 5, 0:C], meta[:, o, 0:1], None, ALU.mult).then_inc(idx_ready, 1)
                dve.wait_ge(idx_ready, t)
                dve.scalar_tensor_tensor(idx[:, o:o + 1], meta[:, o, 1:2], -1.0, idx_f[:, o, 0:1], ALU.add, ALU.add).then_inc(ry_ready, 1)

            def routed(t, par, last=False):
                if last:
                    finish(t, par)
                    return
                tile_in_T(t + 1, 1 - par)
                if not past(t, 0):
                    e = expert_of(dve, 0)
                    with dve.If(e > EARLY - 1):
                        split_up(0, e, 0)
                if past(t, 0):
                    split_up(t + 1, expert_of(dve, t + 1), 1 - par)
                dve.wait_ge(xsT_ready, t + 1)
                if past(t, 1):
                    dve.wait_ge(ry_ready, t - 1)
                dve.tensor_copy(meta[:, par, :], meta_in[:, par, :])
                dve.wait_ge(rsilu_ready, t + 1)
                dve.tensor_tensor(h_rt[:, 0:IM], silu[:, 0:IM], ps_flat[:, IM:2 * IM], ALU.mult)
                dve.tensor_tensor(h_rt[:, IM:I], silu[:, IM:I], ps_flat[:, 2 * IM + IR:W13], ALU.mult).then_inc(rh_ready, 1)
                if past(t, 0):
                    finish(t, par)
                else:
                    dve.wait_ge(base_stored, 16 * CHUNKS)
                    split_up(1, expert_of(dve, 1), 1)

            used = tiles_in_use(dve)
            each_tile(dve, routed, used)


def lay_expert(w1, w2, w3):
    up = np.concatenate([w1[:IM], w3[:IM], w1[IM:], w3[IM:]]).T
    down = np.zeros((IC * 128, C), w2.dtype)
    down[:I] = w2.T
    return np.concatenate([up.reshape(CC, 128, W13).transpose(1, 0, 2).reshape(128, -1),
                           down.reshape(IC, 128, C).transpose(1, 0, 2).reshape(128, -1)], axis=1)


def kernel(**inputs):
    import numpy as _np
    import concourse.bacc as _bacc
    from concourse import mybir as _mybir
    from concourse.bass_utils import run_bass_kernel_spmd as _run
    nc = _bacc.Bacc("TRN2", target_bir_lowering=False, num_devices=1)
    a = {k: _np.asarray(v) for k, v in inputs.items()}
    yT = _np.zeros((CTX, B, LKA), a["ctx_768"].dtype)
    yT[:, :, :LKV] = a["ctx_768"].transpose(2, 0, 1)
    wkv = a["L0_xattn_Wkv"].reshape(CTX, 2, HD)
    arrays = {
        "x": a["x"],
        "ylay": _np.stack([yT[:128], _np.concatenate([yT[128:], yT[128:]])], axis=2),
        "wq": a["L0_xattn_Wq"],
        "wkv": _np.stack([wkv[:128], _np.concatenate([wkv[128:], wkv[128:]])], axis=2),
        "wproj": a["L0_xattn_Wproj"], "bproj": a["L0_xattn_bproj"],
        "eye": _np.eye(128, dtype=_np.float32),
        "router": a["L0_ffn_router_w"].T, "rbias": a["L0_ffn_routing_bias"],
        "experts": _np.stack([lay_expert(*(a[f"L0_ffn_sw{i}"] for i in (1, 2, 3)))]
                             + [lay_expert(*(a[f"L0_ffn_ew{i}"][e] for i in (1, 2, 3))) for e in range(E)]),
        "consts": constants(),
    }
    arrays = {k: _np.ascontiguousarray(v) for k, v in arrays.items()}
    args = [nc.dram_tensor(k, v.shape, _mybir.dt.from_np(v.dtype), kind="ExternalInput").ap() for k, v in arrays.items()]
    out = nc.dram_tensor("out", (B, LQ, C), F32, kind="ExternalOutput").ap()
    build(nc, *args, out)
    r = _run(nc, [arrays], core_ids=[0])
    return r.results[0]["out"]
```
